# Optimizing a Trainium2 kernel written in Bass

```python
import numpy as np
import jax
import jax.numpy as jnp

def _softmax(x, axis=-1):
    return jax.nn.softmax(x, axis=axis)

def _gelu(x):
    return jax.nn.gelu(x, approximate=True)

def _silu(x):
    return jax.nn.silu(x)

def _sigmoid(x):
    return jax.nn.sigmoid(x)

def _layernorm(x, axis=-1, eps=1e-05):
    m = jnp.mean(x, axis=axis, keepdims=True)
    v = jnp.var(x, axis=axis, keepdims=True)
    return (x - m) / jnp.sqrt(v + eps)

def _scatter_add(tgt, idx, src, axis=0):
    return tgt.at[idx].add(src)

def _segment_sum(src, seg, n):
    return jax.ops.segment_sum(src, seg, n)
kernel_name = 'mk_vit_tower_cls_d1_tok_img256_r4_ed4031'

def setup_inputs(seed: int=0):
    np.random.seed(seed)
    _w = jnp.asarray

    def _rec_inputs():
        import jax
        import jax.numpy as jnp
        _rk = jax.random.key(seed)
        x = -0.000520686 + 1.00062 * jax.random.normal(jax.random.fold_in(_rk, 1), (128, 64, 64, 4), jnp.float32)
        cls_tok = 0.02 * jax.random.normal(jax.random.fold_in(_rk, 5), (1, 1, 64), jnp.float32)
        return (x, cls_tok)
    x, cls_tok = _rec_inputs()

    def _L0_tok_setup():
        import jax, jax.numpy as jnp
        import numpy as np
        HIDDEN_DIM = 128
        key = jax.random.key(seed)
        k_geom, k_w, k_b = jax.random.split(key, 3)
        B, N, F = (8, 64, 4)
        geom = jax.random.normal(k_geom, (B, N, N, F), dtype=jnp.float32)
        bound = 1.0 / np.sqrt(F)
        W = jax.random.uniform(k_w, (HIDDEN_DIM, F), dtype=jnp.float32, minval=-bound, maxval=bound)
        b = jax.random.uniform(k_b, (HIDDEN_DIM,), dtype=jnp.float32, minval=-bound, maxval=bound)
        return {'geom': geom, 'W': W, 'b': b}
    _L0_tok_all = _L0_tok_setup()
    _L0_tok_in = {k: v for k, v in _L0_tok_all.items() if k in ('W', 'b')}
    del _L0_tok_all

    def _L0_attn_setup():
        import jax, jax.numpy as jnp
        import numpy as np
        B0, L0, C0 = (4, 144, 64)
        DST, DCONV, EXP = (48, 4, 2)
        DIN = EXP * C0
        DTR = C0 // 16
        FD = 2 * C0

        def _ln(x, g, b, eps=0.001):
            m = jnp.mean(x, -1, keepdims=True)
            v = jnp.mean((x - m) ** 2, -1, keepdims=True)
            return (x - m) / jnp.sqrt(v + eps) * g + b

        def _selective_scan(u, delta, A, Bm, Cm, D):
            dA = jnp.einsum('bld,dn->bldn', delta, A)
            dB_u = jnp.einsum('bld,bld,bln->bldn', delta, u, Bm)
            shifted = jnp.pad(dA[:, 1:], ((0, 0), (1, 1), (0, 0), (0, 0)))[:, 1:]
            dA_cumsum = jnp.exp(jnp.cumsum(shifted[:, ::-1], axis=1))[:, ::-1]
            xs = jnp.cumsum(dB_u * dA_cumsum, axis=1) / (dA_cumsum + 1e-12)
            y = jnp.einsum('bldn,bln->bld', xs, Cm)
            return y + u * D

        def _forward(x, ln1_g, ln1_b, mln_g, mln_b, w_in, conv_w, conv_b, w_xproj, w_dt, b_dt, A_log, D, w_out, ln2_g, ln2_b, fc1_w, bn1_s, bn1_b, Wr, Wi, rb, ib, fc2_w, bn2_s, bn2_b):
            h = _ln(_ln(x, ln1_g, ln1_b), mln_g, mln_b)
            xr = h @ w_in
            xm, res = (xr[..., :DIN], xr[..., DIN:])
            xp = jnp.pad(xm, ((0, 0), (DCONV - 1, 0), (0, 0)))
            xc = jax.lax.conv_general_dilated(xp, conv_w[:, None, :], (1,), 'VALID', dimension_numbers=('NLC', 'LIO', 'NLC'), feature_group_count=DIN) + conv_b
            xc = jax.nn.silu(xc)
            A = -jnp.exp(A_log)
            x_dbl = xc @ w_xproj
            dt, Bm, Cm = (x_dbl[..., :DTR], x_dbl[..., DTR:DTR + DST], x_dbl[..., DTR + DST:])
            delta = jax.nn.softplus(dt @ w_dt + b_dt)
            y = _selective_scan(xc, delta, A, Bm, Cm, D)
            y = y * jax.nn.silu(res)
            x = x + y @ w_out
            h2 = _ln(x, ln2_g, ln2_b)
            f = jax.nn.relu(h2 @ fc1_w * bn1_s + bn1_b)
            L = f.shape[1]
            scale = L ** 0.5
            fr = jnp.fft.rfft(f, axis=1)
            real, imag = (fr.real / scale, fr.imag / scale)
            xre = jax.nn.relu(jnp.einsum('bnc,cd->bnd', real, Wr) - jnp.einsum('bnc,cd->bnd', imag, Wi) + rb)
            xim = jax.nn.relu(jnp.einsum('bnc,cd->bnd', imag, Wr) + jnp.einsum('bnc,cd->bnd', real, Wi) + ib)
            ff = jnp.fft.irfft((xre + 1j * xim) * scale, n=L, axis=1)
            out2 = ff @ fc2_w * bn2_s + bn2_b
            return x + out2
        key = jax.random.key(seed)
        ks = iter(jax.random.split(key, 32))

        def n(shape, s=0.02):
            return jax.random.normal(next(ks), shape, dtype=jnp.float32) * s
        return {'x': jax.random.normal(next(ks), (B0, L0, C0), dtype=jnp.float32), 'ln1_g': jnp.ones((C0,), jnp.float32), 'ln1_b': jnp.zeros((C0,), jnp.float32), 'mln_g': jnp.ones((C0,), jnp.float32), 'mln_b': jnp.zeros((C0,), jnp.float32), 'w_in': n((C0, DIN * EXP)), 'conv_w': n((DCONV, DIN)), 'conv_b': jnp.zeros((DIN,), jnp.float32), 'w_xproj': n((DIN, DTR + 2 * DST)), 'w_dt': n((DTR, DIN)), 'b_dt': jnp.zeros((DIN,), jnp.float32), 'A_log': jnp.log(jnp.tile(jnp.arange(1, DST + 1, dtype=jnp.float32), (DIN, 1))), 'D': jnp.ones((DIN,), jnp.float32), 'w_out': n((DIN, C0)), 'ln2_g': jnp.ones((C0,), jnp.float32), 'ln2_b': jnp.zeros((C0,), jnp.float32), 'fc1_w': n((C0, FD)), 'bn1_s': jnp.ones((FD,), jnp.float32), 'bn1_b': jnp.zeros((FD,), jnp.float32), 'Wr': n((FD, FD)), 'Wi': n((FD, FD)), 'rb': n((FD,)), 'ib': n((FD,)), 'fc2_w': n((FD, C0)), 'bn2_s': jnp.ones((C0,), jnp.float32), 'bn2_b': jnp.zeros((C0,), jnp.float32)}
    _L0_attn_all = _L0_attn_setup()
    _L0_attn_in = {k: v for k, v in _L0_attn_all.items() if k in ('ln1_g', 'ln1_b', 'mln_g', 'mln_b', 'w_in', 'conv_w', 'conv_b', 'w_xproj', 'w_dt', 'b_dt', 'A_log', 'D', 'w_out', 'ln2_g', 'ln2_b', 'fc1_w', 'bn1_s', 'bn1_b', 'Wr', 'Wi', 'rb', 'ib', 'fc2_w', 'bn2_s', 'bn2_b')}
    del _L0_attn_all

    def _L0_ffn_setup():
        import jax, jax.numpy as jnp
        import numpy as np
        NUM_EXPERTS = 8
        TOP_K = 2
        B, S, D = (8, 2048, 64)

        def _moe(tokens, router_w, w1, b1, w2, b2):
            N = tokens.shape[0]
            E = router_w.shape[0]
            logits = tokens.astype(jnp.float32) @ router_w.astype(jnp.float32).T
            probs = jax.nn.softmax(logits, axis=-1)
            rw, re = jax.lax.top_k(probs, TOP_K)
            if TOP_K > 1:
                rw = rw / jnp.maximum(rw.sum(-1, keepdims=True), 1e-12)
            rw = rw.astype(tokens.dtype)
            combine = jnp.zeros((N, E), tokens.dtype).at[jnp.arange(N)[:, None], re].set(rw)
            out = tokens
            for e in range(E):
                h = jax.nn.gelu(tokens @ w1[e] + b1[e], approximate=False)
                y = h @ w2[e] + b2[e]
                out = out + combine[:, e:e + 1] * y
            return out
        key = jax.random.key(seed)
        ks = jax.random.split(key, 4)
        scale = 1.0 / np.sqrt(D).astype(np.float32)
        return {'input_embeddings': jax.random.normal(ks[0], (B, S, D), jnp.float32), 'router_w': jax.random.normal(ks[1], (NUM_EXPERTS, D), jnp.float32) * scale, 'w1': jax.random.normal(ks[2], (NUM_EXPERTS, D, D), jnp.float32) * scale, 'b1': jnp.zeros((NUM_EXPERTS, D), jnp.float32), 'w2': jax.random.normal(ks[3], (NUM_EXPERTS, D, D), jnp.float32) * scale, 'b2': jnp.zeros((NUM_EXPERTS, D), jnp.float32)}
    _L0_ffn_all = _L0_ffn_setup()
    _L0_ffn_in = {k: v for k, v in _L0_ffn_all.items() if k in ('router_w', 'w1', 'b1', 'w2', 'b2')}
    del _L0_ffn_all
    return {'x': x, 'cls_tok': cls_tok, 'L0_tok_W': _L0_tok_in['W'], 'L0_tok_b': _L0_tok_in['b'], 'L0_attn_ln1_g': _L0_attn_in['ln1_g'], 'L0_attn_ln1_b': _L0_attn_in['ln1_b'], 'L0_attn_mln_g': _L0_attn_in['mln_g'], 'L0_attn_mln_b': _L0_attn_in['mln_b'], 'L0_attn_w_in': _L0_attn_in['w_in'], 'L0_attn_conv_w': _L0_attn_in['conv_w'], 'L0_attn_conv_b': _L0_attn_in['conv_b'], 'L0_attn_w_xproj': _L0_attn_in['w_xproj'], 'L0_attn_w_dt': _L0_attn_in['w_dt'], 'L0_attn_b_dt': _L0_attn_in['b_dt'], 'L0_attn_A_log': _L0_attn_in['A_log'], 'L0_attn_D': _L0_attn_in['D'], 'L0_attn_w_out': _L0_attn_in['w_out'], 'L0_attn_ln2_g': _L0_attn_in['ln2_g'], 'L0_attn_ln2_b': _L0_attn_in['ln2_b'], 'L0_attn_fc1_w': _L0_attn_in['fc1_w'], 'L0_attn_bn1_s': _L0_attn_in['bn1_s'], 'L0_attn_bn1_b': _L0_attn_in['bn1_b'], 'L0_attn_Wr': _L0_attn_in['Wr'], 'L0_attn_Wi': _L0_attn_in['Wi'], 'L0_attn_rb': _L0_attn_in['rb'], 'L0_attn_ib': _L0_attn_in['ib'], 'L0_attn_fc2_w': _L0_attn_in['fc2_w'], 'L0_attn_bn2_s': _L0_attn_in['bn2_s'], 'L0_attn_bn2_b': _L0_attn_in['bn2_b'], 'L0_ffn_router_w': _L0_ffn_in['router_w'], 'L0_ffn_w1': _L0_ffn_in['w1'], 'L0_ffn_b1': _L0_ffn_in['b1'], 'L0_ffn_w2': _L0_ffn_in['w2'], 'L0_ffn_b2': _L0_ffn_in['b2']}

def reference(x, cls_tok, L0_tok_W, L0_tok_b, L0_attn_ln1_g, L0_attn_ln1_b, L0_attn_mln_g, L0_attn_mln_b, L0_attn_w_in, L0_attn_conv_w, L0_attn_conv_b, L0_attn_w_xproj, L0_attn_w_dt, L0_attn_b_dt, L0_attn_A_log, L0_attn_D, L0_attn_w_out, L0_attn_ln2_g, L0_attn_ln2_b, L0_attn_fc1_w, L0_attn_bn1_s, L0_attn_bn1_b, L0_attn_Wr, L0_attn_Wi, L0_attn_rb, L0_attn_ib, L0_attn_fc2_w, L0_attn_bn2_s, L0_attn_bn2_b, L0_ffn_router_w, L0_ffn_w1, L0_ffn_b1, L0_ffn_w2, L0_ffn_b2):
    import jax
    import jax.numpy as jnp

    def _L0_tok_ref(geom, W, b):
        import jax, jax.numpy as jnp
        import numpy as np
        HIDDEN_DIM = 128
        bias = jnp.einsum('bijf,hf->bijh', geom, W) + b
        return bias.mean(-1)

    def _L0_attn_ref(x, ln1_g, ln1_b, mln_g, mln_b, w_in, conv_w, conv_b, w_xproj, w_dt, b_dt, A_log, D, w_out, ln2_g, ln2_b, fc1_w, bn1_s, bn1_b, Wr, Wi, rb, ib, fc2_w, bn2_s, bn2_b):
        import jax, jax.numpy as jnp
        import numpy as np
        B0, L0, C0 = (4, 144, 64)
        DST, DCONV, EXP = (48, 4, 2)
        DIN = EXP * C0
        DTR = C0 // 16
        FD = 2 * C0

        def _ln(x, g, b, eps=0.001):
            m = jnp.mean(x, -1, keepdims=True)
            v = jnp.mean((x - m) ** 2, -1, keepdims=True)
            return (x - m) / jnp.sqrt(v + eps) * g + b

        def _selective_scan(u, delta, A, Bm, Cm, D):
            dA = jnp.einsum('bld,dn->bldn', delta, A)
            dB_u = jnp.einsum('bld,bld,bln->bldn', delta, u, Bm)
            shifted = jnp.pad(dA[:, 1:], ((0, 0), (1, 1), (0, 0), (0, 0)))[:, 1:]
            dA_cumsum = jnp.exp(jnp.cumsum(shifted[:, ::-1], axis=1))[:, ::-1]
            xs = jnp.cumsum(dB_u * dA_cumsum, axis=1) / (dA_cumsum + 1e-12)
            y = jnp.einsum('bldn,bln->bld', xs, Cm)
            return y + u * D

        def _forward(x, ln1_g, ln1_b, mln_g, mln_b, w_in, conv_w, conv_b, w_xproj, w_dt, b_dt, A_log, D, w_out, ln2_g, ln2_b, fc1_w, bn1_s, bn1_b, Wr, Wi, rb, ib, fc2_w, bn2_s, bn2_b):
            h = _ln(_ln(x, ln1_g, ln1_b), mln_g, mln_b)
            xr = h @ w_in
            xm, res = (xr[..., :DIN], xr[..., DIN:])
            xp = jnp.pad(xm, ((0, 0), (DCONV - 1, 0), (0, 0)))
            xc = jax.lax.conv_general_dilated(xp, conv_w[:, None, :], (1,), 'VALID', dimension_numbers=('NLC', 'LIO', 'NLC'), feature_group_count=DIN) + conv_b
            xc = jax.nn.silu(xc)
            A = -jnp.exp(A_log)
            x_dbl = xc @ w_xproj
            dt, Bm, Cm = (x_dbl[..., :DTR], x_dbl[..., DTR:DTR + DST], x_dbl[..., DTR + DST:])
            delta = jax.nn.softplus(dt @ w_dt + b_dt)
            y = _selective_scan(xc, delta, A, Bm, Cm, D)
            y = y * jax.nn.silu(res)
            x = x + y @ w_out
            h2 = _ln(x, ln2_g, ln2_b)
            f = jax.nn.relu(h2 @ fc1_w * bn1_s + bn1_b)
            L = f.shape[1]
            scale = L ** 0.5
            fr = jnp.fft.rfft(f, axis=1)
            real, imag = (fr.real / scale, fr.imag / scale)
            xre = jax.nn.relu(jnp.einsum('bnc,cd->bnd', real, Wr) - jnp.einsum('bnc,cd->bnd', imag, Wi) + rb)
            xim = jax.nn.relu(jnp.einsum('bnc,cd->bnd', imag, Wr) + jnp.einsum('bnc,cd->bnd', real, Wi) + ib)
            ff = jnp.fft.irfft((xre + 1j * xim) * scale, n=L, axis=1)
            out2 = ff @ fc2_w * bn2_s + bn2_b
            return x + out2
        return _forward(x, ln1_g, ln1_b, mln_g, mln_b, w_in, conv_w, conv_b, w_xproj, w_dt, b_dt, A_log, D, w_out, ln2_g, ln2_b, fc1_w, bn1_s, bn1_b, Wr, Wi, rb, ib, fc2_w, bn2_s, bn2_b)

    def _L0_ffn_ref(input_embeddings, router_w, w1, b1, w2, b2):
        import jax, jax.numpy as jnp
        import numpy as np
        NUM_EXPERTS = 8
        TOP_K = 2
        B, S, D = (8, 2048, 64)

        def _moe(tokens, router_w, w1, b1, w2, b2):
            N = tokens.shape[0]
            E = router_w.shape[0]
            logits = tokens.astype(jnp.float32) @ router_w.astype(jnp.float32).T
            probs = jax.nn.softmax(logits, axis=-1)
            rw, re = jax.lax.top_k(probs, TOP_K)
            if TOP_K > 1:
                rw = rw / jnp.maximum(rw.sum(-1, keepdims=True), 1e-12)
            rw = rw.astype(tokens.dtype)
            combine = jnp.zeros((N, E), tokens.dtype).at[jnp.arange(N)[:, None], re].set(rw)
            out = tokens
            for e in range(E):
                h = jax.nn.gelu(tokens @ w1[e] + b1[e], approximate=False)
                y = h @ w2[e] + b2[e]
                out = out + combine[:, e:e + 1] * y
            return out
        b, s, d = input_embeddings.shape
        tokens = input_embeddings.reshape(b * s, d)
        return _moe(tokens, router_w, w1, b1, w2, b2).reshape(b, s, d)
    h = _L0_tok_ref(x, L0_tok_W, L0_tok_b)
    h = jnp.concatenate([jnp.broadcast_to(cls_tok, (h.shape[0], 1, h.shape[2])), h], axis=1)
    h = h + _L0_attn_ref(_layernorm(h, axis=-1), L0_attn_ln1_g, L0_attn_ln1_b, L0_attn_mln_g, L0_attn_mln_b, L0_attn_w_in, L0_attn_conv_w, L0_attn_conv_b, L0_attn_w_xproj, L0_attn_w_dt, L0_attn_b_dt, L0_attn_A_log, L0_attn_D, L0_attn_w_out, L0_attn_ln2_g, L0_attn_ln2_b, L0_attn_fc1_w, L0_attn_bn1_s, L0_attn_bn1_b, L0_attn_Wr, L0_attn_Wi, L0_attn_rb, L0_attn_ib, L0_attn_fc2_w, L0_attn_bn2_s, L0_attn_bn2_b)
    h = h + _L0_ffn_ref(_layernorm(h, axis=-1), L0_ffn_router_w, L0_ffn_w1, L0_ffn_b1, L0_ffn_w2, L0_ffn_b2)
    return h

_drawn_inputs = setup_inputs


def setup_inputs(seed=0):
    import zlib

    import numpy as np

    out = dict(_drawn_inputs(seed))
    spreads = {'L0_attn_ln1_g': (1.0, 0.6),
     'L0_attn_ln1_b': (0.0, 0.8),
     'L0_attn_mln_g': (1.0, 0.6),
     'L0_attn_mln_b': (0.0, 0.8),
     'L0_attn_conv_b': (0.0, 0.8),
     'L0_attn_b_dt': (0.0, 0.8),
     'L0_attn_D': (1.0, 0.6),
     'L0_attn_ln2_g': (1.0, 0.6),
     'L0_attn_ln2_b': (0.0, 0.8),
     'L0_attn_bn1_s': (1.0, 0.6),
     'L0_attn_bn1_b': (0.0, 0.66),
     'L0_attn_bn2_s': (1.0, 0.6),
     'L0_attn_bn2_b': (0.0, 0.5),
     'L0_ffn_b1': (0.0, 1.399),
     'L0_ffn_b2': (0.0, 0.8)}
    factors = {'L0_tok_b': 64.0,
     'L0_attn_w_in': 8.0,
     'L0_attn_conv_w': 8.0,
     'L0_attn_w_xproj': 8.0,
     'L0_attn_w_dt': 8.0,
     'L0_attn_A_log': 8.0,
     'L0_attn_w_out': 8.0,
     'L0_attn_fc1_w': 5.031,
     'L0_attn_Wr': 4.688,
     'L0_attn_Wi': 5.941,
     'L0_attn_rb': 21.739,
     'L0_attn_ib': 20.981,
     'L0_attn_fc2_w': 3.971}
    for name, (base, spread) in spreads.items():
        noise = np.random.default_rng([zlib.crc32(name.encode()), seed]).standard_normal(out[name].shape)
        drawn = base * np.exp(spread * noise) if base else spread * noise
        out[name] = jnp.asarray(drawn.astype(out[name].dtype))
    for name, factor in factors.items():
        out[name] = (out[name] * factor).astype(out[name].dtype)
    return out
```

```python
from contextlib import ExitStack

import concourse.bass as bass
from concourse import mybir

F32 = mybir.dt.float32
BF16 = mybir.dt.bfloat16
ALU = mybir.AluOpType
ACT = mybir.ActivationFunctionType
AX_X = mybir.AxisListType.X

NIMG, GRID, CH = 128, 64, 64
NF = 4
L = GRID + 1
DIN = 2 * CH
DTR, DST, DCONV = CH // 16, 48, 4
NE = 8
NFREQ = L // 2 + 1
BI = 16
HI = BI // 2
NBLK = NIMG // BI
T = BI * L
TH = HI * L
Q = T // 4
IQ = BI // 4
NG, GR = 3, 16
BANK = 512
HALF_LN = 13.815510557964274

PACK = dict(
    tok=(NF + 1, 128), ident=(128, 128), center=(128, 128), avg=(128, 128), w_in=(256, 128), conv_w=(DCONV, 128),
    conv_b=(1, 128), b_dt=(1, 128), D=(1, 128), rb=(1, 128), ib=(1, 128), ln1_g=(1, 128), ln1_b=(1, 128),
    mln_g=(1, 128), mln_b=(1, 128), ln2_g=(1, 128), ln2_b=(1, 128), bn2_s=(1, 128), bn2_b=(1, 128), cls=(1, 128),
    b1=(4, 128), A_log=(DST, 128), w_dtr=(DTR, 128), w_bc=(NG * 96, 128), w_dt=(128, DTR), onehot=(32, 96),
    w_out=(CH, 128), fc1=(128, 128), bn1_s=(128, 128), bn1_b=(BANK, 1), Wr=(128, 128), Wi=(128, 128),
    fc2=(CH, 128), dft=(2 * NFREQ, L), idft=(L, 2 * NFREQ), router=(NE, 128), w1=(4 * 128, 128), w2=(4 * CH, 128),
    b2=(CH, NE), pick=(4 * 128, NE), rank=(NE, 128))
PACK_AT = {}
_at = 0
for _name, (_w, _) in PACK.items():
    PACK_AT[_name] = _at
    _at += _w
PACK_COLS = _at


def build(nc, x, packed, out):
    with ExitStack() as ctx:
        def sb(name, shape, dt=F32):
            return ctx.enter_context(nc.sbuf_tensor(name, shape, dt))

        def sem(name):
            return ctx.enter_context(nc.semaphore(name))

        pack = sb("pack", [128, PACK_COLS])

        def w(name):
            cols, rows = PACK[name]
            return pack[0:rows, PACK_AT[name]:PACK_AT[name] + cols]

        eps_col = sb("eps_col", [128, 4])
        mean_h = sb("mean_h", [128, 128])
        tokw = sb("tokw", [128, NF + 1])
        Aneg = sb("Aneg", [128, DST])
        Ahalf = sb("Ahalf", [128, DST])
        Aexp = sb("Aexp", [128, DST])
        half_ident = sb("half_ident", [128, 128])
        diagD = sb("diagD", [128, 128])
        diag_conv = sb("diag_conv", [128, DCONV, 128])
        conv_bh = sb("conv_bh", [128, 1])
        w_out_half = sb("w_out_half", [128, CH])
        fc1s = sb("fc1s", [128, 128])
        negWi = sb("negWi", [128, 128])
        sel = sb("sel", [96, 32, 128], BF16)
        ones_row = sb("ones_row", [1, L])
        not_last = sb("not_last", [128, BI, L])

        xin = sb("xin", [128, 4, 2, CH * NF])
        tokT = sb("tokT", [128, 2 * 4, CH])
        H = sb("H", [128, TH])
        ln_sq = sb("ln_sq", [128, TH])
        ln_r = sb("ln_r", [128, TH])
        ln_y = sb("ln_y", [128, TH])
        x0 = sb("x0", [128, TH])
        h1 = sb("h1", [128, TH])
        h2 = sb("h2", [128, TH])
        xm_pad = sb("xm_pad", [128, BI, L + DCONV - 1])
        th = sb("th", [128, T])
        gate2 = sb("gate2", [128, T])
        vh = sb("vh", [128, T])
        u = sb("u", [128, T])
        dts = sb("dts", [DTR, T])
        s_relu = sb("s_relu", [128, T])
        s_abs = sb("s_abs", [128, T])
        s_exp = sb("s_exp", [128, T])
        s_log = sb("s_log", [128, T])
        delta = sb("delta", [128, T + 1])
        dsum = sb("dsum", [128, T])
        du = sb("du", [128, T])
        pf = sb("pf", [64, NG, T])
        rest = sb("rest", [64, T])
        stack = sb("stack", [96, NG, T], BF16)
        a = sb("a", [128, 2, BI, L])
        m = sb("m", [128, 2, T])
        dBu = sb("dBu", [128, 2, T])
        q = sb("q", [128, 2, T])
        xs = sb("xs", [128, 2, T])
        z = sb("z", [128, 2, T])
        yg = s_relu
        x1 = h1
        h3 = h2
        def whole(t3d):
            return t3d[:, :, :].rearrange("p a b -> p (a b)")

        fT = whole(q)[0:L, 0:4 * BANK]
        ri = whole(xs)[:, 0:BI * 2 * NFREQ].rearrange("p (b c) -> p b c", b=4)
        xx = whole(m)[:, 0:BI * 2 * NFREQ].rearrange("p (e f) -> p e f", e=BI)
        gmat = whole(m)[0:2 * NFREQ, BI * 2 * NFREQ:BI * 2 * NFREQ + 2 * BANK]
        hx = sb("hx", [128, TH])
        ff = sb("ff", [128, TH])
        hA = sb("hA", [128, TH])
        xf = sb("xf", [128, TH])
        lg = sb("lg", [L, BI, NE])
        lg2 = sb("lg2", [L, BI, NE])
        eq = sb("eq", [L, BI, NE])
        key = sb("key", [L, BI, NE])
        oh1 = sb("oh1", [L, BI, NE])
        oh2 = sb("oh2", [L, BI, NE])
        stat = sb("stat", [L, 8, BI])
        comb = sb("comb", [L, BI, NE])
        combT = th[0:NE, :]
        hid = z[:, 0, :].rearrange("p (k c) -> p k c", k=2)
        gated = z[:, 1, :].rearrange("p (k c) -> p k c", k=2)
        fin = vh[:, 0:TH]
        outT = sb("outT", [L, HI, 2, CH])

        ps = ctx.enter_context(nc.psum_tensor("ps", [128, 8, BANK], F32))
        flat = ps[:, :, :].rearrange("p b c -> p (b c)")
        Y0, B0, C0 = 0, 3 * BANK, 3 * BANK + T
        psY, psB, psC = (flat[:, o:o + T] for o in (Y0, B0, C0))

        def pieces(start):
            o = start
            while o < start + T:
                e = min(start + T, (o // BANK + 1) * BANK)
                yield o, o - start, e - o
                o = e

        def quarters(t2d):
            return t2d.rearrange("p (k c) -> p k c", c=Q)

        names = """packed_in x_in prep_wait prepped memset_done tok_mean tokw_ready A_exp tok_step h_turned h_ready
            ln_centered ln_squared ln_var ln_log ln_rstd ln_scaled ln_done xm_ready res_ready xm_padded res_tanh
            gate_ready conv_ready conv_tanh conv_half u_ready dt_ready dts_ready v_ready soft_relu soft_abs soft_exp
            soft_log soft_step du_ready dsum_ready bc_ready bc_copied split_step
            a_ready m_ready BC_ready dBu_ready x_done q_done z_done y_added
            yg_ready proj_ready x1_ready f_ready fT_ready dft_ready ri_ready mix_ready xx_ready fc2_ready gmat_ready
            ff_ready ff_scaled hx_ready hA_ready hx2_ready logits_ready route_step pair_exp comb_turned combT_ready
            hid_ready hid_done bcast_ready gated_ready acc_done fin_ready out_turned outT_ready out_stored"""
        s = {n: sem(n) for n in names.split()}
        NPREP = 12
        NBUF = 2
        LNS = 5
        RS = 19
        MS = 8

        x_v = x.rearrange("(n h k e) i j f -> n (e i) k h (j f)", n=NBLK, h=2, k=4)
        out_v = out.rearrange("(n h e) l c -> n h l e c", n=NBLK, h=2)

        block = ctx.enter_context(nc.Block())

        @block.sync
        def _(sp):
            sp.dma_start(pack[:, :], packed).then_inc(s["packed_in"], 16)
            with sp.Fori(0, NBLK) as i:
                sp.wait_ge(s["tok_step"], i * 4 + 1)
                for h in range(2):
                    sp.dma_start(xin[:, :, h, :], x_v[i, :, :, h, :]).then_inc(s["x_in"], 16)
                sp.wait_ge(s["outT_ready"], i + 2)
                for h in range(2):
                    sp.dma_start(out_v[i, h], outT[:, :, h, :]).then_inc(s["out_stored"], 16)
            sp.wait_ge(s["out_stored"], 32 * NBLK + 1)

        @block.gpsimd
        def _(pool):
            for k, v in enumerate((1e-5, 1e-3, 1.0, HALF_LN)):
                pool.memset(eps_col[:, k:k + 1], v).then_inc(s["memset_done"], 1)
            pool.memset(mean_h[:, :], 1.0 / 128).then_inc(s["memset_done"], 1)
            pool.memset(ones_row[:, :], 1.0).then_inc(s["memset_done"], 1)
            pool.memset(delta[:, T:T + 1], 0.0).then_inc(s["memset_done"], 1)
            pool.memset(xm_pad[:, :, 0:DCONV - 1], 0.0).then_inc(s["memset_done"], 1)
            pool.memset(not_last[:, :, 0:L - 1], 1.0).then_inc(s["memset_done"], 1)
            pool.memset(not_last[:, :, L - 1:L], 0.0).then_inc(s["memset_done"], 1)
            pool.memset(tokT[:, 0, 0:1], 0.0).then_inc(s["tok_step"], 1)
            pool.memset(outT[:, 0, 0, 0:1], 0.0).then_inc(s["outT_ready"], 1)
            pool.memset(outT[:, 0, 0, 1:2], 0.0).then_inc(s["out_stored"], 1)
            for p in range(NBUF):
                pool.memset(a[:, p, :, 0:1], 0.0).then_inc(s["x_done"], 1)
                pool.memset(m[:, p, 0:1], 0.0).then_inc(s["q_done"], 1)
                pool.memset(xs[:, p, 0:1], 0.0).then_inc(s["z_done"], 1)
                pool.memset(z[:, p, 0:1], 0.0).then_inc(s["y_added"], 1)
            with pool.Fori(0, NBLK) as i:
                pool.wait_ge(s["soft_step"], i * 4 + 1)
                pool.tensor_tensor(s_abs[:, :], s_exp[:, :], s_abs[:, :], ALU.subtract).then_inc(s["soft_step"], 1)
                pool.wait_ge(s["soft_step"], i * 4 + 2)
                pool.wait_ge(s["soft_log"], i + 1)
                pool.tensor_tensor(s_log[:, :], s_abs[:, :], s_log[:, :], ALU.add).then_inc(s["soft_step"], 1)
                pool.wait_ge(s["soft_step"], i * 4 + 3)
                pool.tensor_tensor(delta[:, 0:T], s_log[:, :], s_relu[:, :], ALU.add).then_inc(s["soft_step"], 1)
                pool.wait_ge(s["soft_step"], i * 4 + 4)
                pool.tensor_tensor(du[:, :], delta[:, 0:T], u[:, :], ALU.mult).then_inc(s["du_ready"], 1)
                for g in range(NG):
                    pool.wait_ge(s["bc_copied"], (i * NG + g + 1) * 2)
                    pool.tensor_tensor(rest[:, :], pf[:, g, :], stack[0:64, g, :], ALU.subtract)\
                        .then_inc(s["split_step"], 1)
                    pool.wait_ge(s["split_step"], (i * NG + g) * 3 + 1)
                    pool.tensor_tensor(stack[0:64, g, :], pf[:, g, :], stack[0:64, g, :], ALU.subtract)\
                        .then_inc(s["split_step"], 1)
                    pool.wait_ge(s["split_step"], (i * NG + g) * 3 + 2)
                    pool.tensor_tensor(stack[0:32, g, :], rest[0:32, :], stack[0:32, g, :], ALU.subtract)\
                        .then_inc(s["split_step"], 1)
                    if g < NG - 1:
                        pool.wait_ge(s["split_step"], (i * NG + g) * 3 + 3)
                with pool.Fori(0, DST // 2) as j:
                    for p in range(2):
                        n = i * DST + j * 2 + p
                        pool.wait_ge(s["x_done"], n + 1 + NBUF)
                        pool.wait_ge(s["q_done"], n + 1 + NBUF)
                        pool.wait_ge(s["y_added"], n + 1)
                        pool.tensor_tensor(z[:, p, :], q[:, p, :], xs[:, p, :], ALU.mult)\
                            .then_inc(s["z_done"], 1)
                pool.wait_ge(s["x1_ready"], i + 1)
                pool.tensor_tensor(hx[:, :], H[:, :], x1[:, :], ALU.add).then_inc(s["hx_ready"], 1)
                pool.wait_ge(s["hA_ready"], i + 1)
                pool.wait_ge(s["ln_done"], i * LNS + 5)
                pool.tensor_tensor(hx[:, :], hA[:, :], xf[:, :], ALU.add).then_inc(s["hx2_ready"], 1)

        @block.scalar
        def _(act):
            act.wait_ge(s["packed_in"], 16)
            act.activation(Aexp[:, :], w("A_log"), ACT.Exp).then_inc(s["A_exp"], 1)
            act.wait_ge(s["tok_mean"], 1)
            act.activation(tokw[:, :], ps[:, 0, 0:NF + 1], ACT.Copy).then_inc(s["tokw_ready"], 1)
            act.wait_ge(s["memset_done"], 10)
            act.wait_ge(s["prepped"], NPREP)

            def layer_norm(i, k, eps):
                n = i * LNS + k + 1
                act.wait_ge(s["ln_centered"], n)
                act.activation(ln_sq[:, :].rearrange("p (b c) -> p b c", c=Q), ps[:, 0:2, 0:Q], ACT.Square)\
                    .then_inc(s["ln_squared"], 1)
                act.wait_ge(s["ln_var"], n)
                act.activation(ln_r[:, :].rearrange("p (b c) -> p b c", c=Q), ps[:, 2:4, 0:Q], ACT.Ln,
                               bias=eps_col[:, eps:eps + 1]).then_inc(s["ln_log"], 1)
                act.wait_ge(s["ln_log"], n)
                act.activation(ln_r[:, :], ln_r[:, :], ACT.Exp, scale=-0.5).then_inc(s["ln_rstd"], 1)

            with act.Fori(0, NBLK) as i:
                act.wait_ge(s["h_turned"], i + 1)
                Hv = H[:, :].rearrange("p (e l) -> p e l", l=L)
                act.activation(Hv[:, :, 1:L], ps[:, 0, :].rearrange("p (e l) -> p e l", l=GRID), ACT.Copy)\
                    .then_inc(s["h_ready"], 1)
                for k in range(3):
                    layer_norm(i, k, 0 if k == 0 else 1)
                act.wait_ge(s["xm_ready"], i + 1)
                act.activation(xm_pad[:, :, DCONV - 1:].rearrange("p (k e) l -> p k e l", e=IQ),
                               ps[:, 0:4, 0:Q].rearrange("p k (e l) -> p k e l", l=L), ACT.Copy)\
                    .then_inc(s["xm_padded"], 1)
                act.wait_ge(s["res_ready"], i + 1)
                act.activation(quarters(th[:, :]), ps[:, 4:8, 0:Q], ACT.Tanh, scale=0.5).then_inc(s["res_tanh"], 1)
                act.wait_ge(s["conv_ready"], i + 1)
                act.activation(quarters(vh[:, :]), ps[:, 0:4, 0:Q], ACT.Identity, bias=conv_bh[:, :], scale=0.5)\
                    .then_inc(s["conv_half"], 1)
                act.wait_ge(s["gate_ready"], i + 1)
                act.activation(quarters(th[:, :]), ps[:, 0:4, 0:Q], ACT.Tanh, bias=conv_bh[:, :], scale=0.5)\
                    .then_inc(s["conv_tanh"], 1)
                act.wait_ge(s["dt_ready"], i + 1)
                act.activation(quarters(dts[:, :]), ps[0:DTR, 4:8, 0:Q], ACT.Copy).then_inc(s["dts_ready"], 1)
                act.wait_ge(s["v_ready"], i + 1)
                act.activation(quarters(s_abs[:, :]), ps[:, 0:4, 0:Q], ACT.Abs, bias=w("b_dt")).then_inc(s["soft_abs"], 1)
                act.activation(quarters(s_relu[:, :]), ps[:, 0:4, 0:Q], ACT.Relu, bias=w("b_dt"))\
                    .then_inc(s["soft_relu"], 1)
                act.wait_ge(s["soft_abs"], i + 1)
                act.activation(s_exp[:, :], s_abs[:, :], ACT.Exp, scale=-1.0).then_inc(s["soft_exp"], 1)
                act.wait_ge(s["soft_exp"], i + 1)
                act.activation(s_log[:, :], s_exp[:, :], ACT.Ln, bias=eps_col[:, 2:3]).then_inc(s["soft_log"], 1)
                for g in range(NG):
                    b = 4 if g % 2 == 0 else 0
                    act.wait_ge(s["bc_ready"], i * NG + g + 1)
                    act.activation(quarters(stack[:, g, :]), ps[0:96, b:b + 4, 0:Q], ACT.Copy)\
                        .then_inc(s["bc_copied"], 1)
                    act.activation(quarters(pf[:, g, :]), ps[0:64, b:b + 4, 0:Q], ACT.Copy)\
                        .then_inc(s["bc_copied"], 1)
                act.wait_ge(s["soft_step"], i * 4 + 4)
                act.wait_ge(s["dsum_ready"], i + 1)
                dv = delta[:, 0:T].rearrange("p (e l) -> p e l", l=L)
                with act.Fori(0, DST // 2) as j:
                    for p in range(2):
                        n = i * DST + j * 2 + p
                        col = bass.ds(j * 2 + p, 1)
                        act.wait_ge(s["x_done"], n + 1)
                        act.activation(a[:, p, :, 1:L], dv[:, :, 1:L], ACT.Exp, scale=Aneg[:, col])\
                            .then_inc(s["a_ready"], 1)
                        act.wait_ge(s["q_done"], n + 1)
                        act.activation(m[:, p, :], dsum[:, :], ACT.Tanh, scale=Ahalf[:, col],
                                       bias=eps_col[:, 3:4]).then_inc(s["m_ready"], 1)
                layer_norm(i, 3, 1)
                act.wait_ge(s["f_ready"], i + 1)
                act.activation(fT[:, :].rearrange("p (b c) -> p b c", c=BANK), ps[0:L, 0:4, :], ACT.Relu)\
                    .then_inc(s["fT_ready"], 1)
                act.wait_ge(s["dft_ready"], i + 1)
                act.activation(ri[:, :, :], ps[:, 4:8, 0:4 * 2 * NFREQ], ACT.Copy).then_inc(s["ri_ready"], 1)
                act.wait_ge(s["mix_ready"], i + 1)
                for c, bias in ((0, "rb"), (1, "ib")):
                    act.activation(xx[:, :, c * NFREQ:(c + 1) * NFREQ].rearrange("p (b e) f -> p b e f", b=2),
                                   ps[:, 2 * c:2 * c + 2, 0:8 * NFREQ].rearrange("p b (e f) -> p b e f", f=NFREQ),
                                   ACT.Relu, bias=w(bias)).then_inc(s["xx_ready"], 1)
                act.wait_ge(s["fc2_ready"], i + 1)
                act.activation(gmat[:, :].rearrange("p (b c) -> p b c", c=BANK), ps[0:2 * NFREQ, 4:6, :], ACT.Copy)\
                    .then_inc(s["gmat_ready"], 1)
                layer_norm(i, 4, 0)
                act.wait_ge(s["route_step"], i * RS + 13)
                act.activation(stat[:, 5, :], stat[:, 4, :], ACT.Exp).then_inc(s["pair_exp"], 1)
                act.wait_ge(s["comb_turned"], i + 1)
                act.activation(quarters(combT[:, :]), ps[0:NE, 4:8, 0:Q], ACT.Copy).then_inc(s["combT_ready"], 1)
                for st in range(MS):
                    k, p = st // 2, st % 2
                    act.wait_ge(s["hid_ready"], i * MS + st + 1)
                    if st >= 2:
                        act.wait_ge(s["gated_ready"], i * MS + st - 1)
                    act.activation(hid[:, p, :].rearrange("p (b c) -> p b c", c=Q), ps[:, 2 * p:2 * p + 2, 0:Q],
                                   ACT.Gelu, bias=w("b1")[:, k:k + 1]).then_inc(s["hid_done"], 1)
                act.wait_ge(s["out_turned"], i + 1)
                act.wait_ge(s["out_stored"], 32 * i + 1)
                act.activation(outT[:, :, :, :].rearrange("p (b e) h c -> p b (e h c)", b=2), ps[0:L, 0:2, :], ACT.Copy)\
                    .then_inc(s["outT_ready"], 1)

        @block.vector
        def _(dve):
            dve.wait_ge(s["packed_in"], 16)
            dve.wait_ge(s["A_exp"], 1)
            dve.tensor_scalar(Aneg[:, :], Aexp[:, :], -1.0, None, ALU.mult).then_inc(s["prepped"], 1)
            dve.tensor_scalar(Ahalf[:, :], Aexp[:, :], -0.5, None, ALU.mult).then_inc(s["prepped"], 1)
            dve.tensor_scalar(half_ident[:, :], w("ident"), 0.5, None, ALU.mult).then_inc(s["prepped"], 1)
            dve.tensor_scalar(diagD[:, :], w("ident"), w("D"), None, ALU.mult).then_inc(s["prepped"], 1)
            for k in range(DCONV):
                dve.tensor_scalar(diag_conv[:, k, :], w("ident"), w("conv_w")[:, k:k + 1], None, ALU.mult)\
                    .then_inc(s["prepped"], 1)
            dve.tensor_scalar(conv_bh[:, :], w("conv_b"), 0.5, None, ALU.mult).then_inc(s["prepped"], 1)
            dve.tensor_scalar(w_out_half[:, :], w("w_out"), 0.5, None, ALU.mult).then_inc(s["prepped"], 1)
            dve.tensor_tensor(fc1s[:, :], w("fc1"), w("bn1_s"), ALU.mult).then_inc(s["prepped"], 1)
            dve.tensor_scalar(negWi[:, :], w("Wi"), -1.0, None, ALU.mult).then_inc(s["prepped"], 1)
            Hv = H[:, :].rearrange("p (e l) -> p e l", l=L)
            dve.tensor_copy(Hv[:, :, 0:1], w("cls").unsqueeze(2).to_broadcast([128, HI, 1])).then_inc(s["prep_wait"], 1)
            dve.tensor_copy(sel[:, :, :], w("onehot").unsqueeze(2).to_broadcast([96, 32, 128]))\
                .then_inc(s["prep_wait"], 1)
            dve.wait_ge(s["tokw_ready"], 1)
            dve.wait_ge(s["memset_done"], 10)

            def two(t2d):
                return t2d.rearrange("p (b c) -> p b c", c=Q)

            def layer_norm(i, k, dst, g=None, b=None, affine=0):
                dve.wait_ge(s["ln_rstd"], i * LNS + k + 1)
                c = ps[:, 0:2, 0:Q]
                if g is None:
                    dve.tensor_tensor(two(dst[:, :]), c, two(ln_r[:, :]), ALU.mult).then_inc(s["ln_done"], 1)
                    return
                dve.scalar_tensor_tensor(two(ln_y[:, :]), c, w(g), two(ln_r[:, :]), ALU.mult, ALU.mult)\
                    .then_inc(s["ln_scaled"], 1)
                dve.wait_ge(s["ln_scaled"], i * 3 + affine + 1)
                dve.tensor_scalar(dst[:, :], ln_y[:, :], w(b), None, ALU.add).then_inc(s["ln_done"], 1)

            with dve.Fori(0, NBLK) as i:
                dve.wait_ge(s["x_in"], i * 32 + 32)
                xv = xin[:, :, :, :].rearrange("p k h (j f) -> p (k h) j f", f=NF)
                dve.tensor_scalar(tokT[:, :, :], xv[:, :, :, 0], tokw[:, 0:1], tokw[:, NF:NF + 1], ALU.mult, ALU.add)\
                    .then_inc(s["tok_step"], 1)
                for f in range(1, NF):
                    dve.wait_ge(s["tok_step"], i * 4 + f + 1)
                    dve.scalar_tensor_tensor(tokT[:, :, :], xv[:, :, :, f], tokw[:, f:f + 1], tokT[:, :, :],
                                             ALU.mult, ALU.add).then_inc(s["tok_step"], 1)
                layer_norm(i, 0, x0)
                layer_norm(i, 1, h1, "ln1_g", "ln1_b", 0)
                layer_norm(i, 2, h2, "mln_g", "mln_b", 1)
                dve.wait_ge(s["res_tanh"], i + 1)
                dve.scalar_tensor_tensor(quarters(gate2[:, :]), quarters(th[:, :]), 1.0, ps[:, 4:8, 0:Q],
                                         ALU.add, ALU.mult).then_inc(s["gate_ready"], 1)
                dve.wait_ge(s["conv_tanh"], i + 1)
                dve.wait_ge(s["conv_half"], i + 1)
                dve.scalar_tensor_tensor(u[:, :], th[:, :], 1.0, vh[:, :], ALU.add, ALU.mult).then_inc(s["u_ready"], 1)
                dve.wait_ge(s["soft_exp"], i + 1)
                dve.tensor_scalar(s_abs[:, :], s_exp[:, :], 1.0, -1.0, ALU.add, ALU.add).then_inc(s["soft_step"], 1)
                dve.wait_ge(s["soft_step"], i * 4 + 4)
                keep = not_last[:, :, :].rearrange("p e l -> p (e l)")
                dve.tensor_tensor_scan(dsum[:, ::-1], delta[:, T:0:-1], keep[:, ::-1], 0.0, ALU.add, ALU.mult)\
                    .then_inc(s["dsum_ready"], 1)
                with dve.Fori(0, DST // 2) as j:
                    for p in range(2):
                        n = i * DST + j * 2 + p
                        dve.wait_ge(s["du_ready"], i + 1)
                        dve.wait_ge(s["BC_ready"], n + 1)
                        dve.wait_ge(s["x_done"], n + 1)
                        dve.tensor_tensor(dBu[:, p, :], psB, du[:, :], ALU.mult).then_inc(s["dBu_ready"], 1)
                        dve.wait_ge(s["m_ready"], n + 1)
                        dve.wait_ge(s["z_done"], n + 1)
                        dve.scalar_tensor_tensor(q[:, p, :], m[:, p, :], 1.0, psC, ALU.add, ALU.mult)\
                            .then_inc(s["q_done"], 1)
                        dve.wait_ge(s["a_ready"], n + 1)
                        dve.wait_ge(s["dBu_ready"], n + 1)
                        dve.tensor_tensor_scan(xs[:, p, :], a[:, p, :, :].rearrange("p e l -> p (e l)"), dBu[:, p, :], 0.0,
                                               ALU.mult, ALU.add).then_inc(s["x_done"], 1)
                dve.wait_ge(s["y_added"], (i + 1) * DST + NBUF)
                dve.tensor_tensor(yg[:, :], psY, gate2[:, :], ALU.mult).then_inc(s["yg_ready"], 1)
                dve.wait_ge(s["proj_ready"], i + 1)
                dve.tensor_tensor(two(x1[:, :]), ps[:, 3:5, 0:Q], two(x0[:, :]), ALU.add).then_inc(s["x1_ready"], 1)
                layer_norm(i, 3, h3, "ln2_g", "ln2_b", 2)
                dve.wait_ge(s["ff_ready"], i + 1)
                dve.tensor_scalar(two(ff[:, :]), ps[:, 0:2, 0:Q], w("bn2_s"), w("bn2_b"), ALU.mult, ALU.add)\
                    .then_inc(s["ff_scaled"], 1)
                dve.wait_ge(s["ff_scaled"], i + 1)
                dve.wait_ge(s["hx_ready"], i + 1)
                dve.tensor_tensor(hA[:, :], ff[:, :], hx[:, :], ALU.add).then_inc(s["hA_ready"], 1)
                layer_norm(i, 4, xf)

                def wide(k):
                    return stat[:, k, :].unsqueeze(2).to_broadcast([L, BI, NE])

                step = [0]

                def then(ins):
                    step[0] += 1
                    ins.then_inc(s["route_step"], 1)
                    dve.wait_ge(s["route_step"], i * RS + step[0])

                rank = w("rank")[0:L, :].unsqueeze(1).to_broadcast([L, BI, NE])
                dve.wait_ge(s["logits_ready"], i + 1)
                then(dve.tensor_copy(lg[:, :, :].rearrange("p (h e) x -> p h (e x)", h=2), ps[0:L, 4:6, 0:HI * NE]))
                then(dve.tensor_reduce(stat[:, 0, :], lg[:, :, :], AX_X, ALU.max))
                then(dve.tensor_tensor(eq[:, :, :], lg[:, :, :], wide(0), ALU.is_equal))
                then(dve.tensor_tensor(key[:, :, :], eq[:, :, :], rank, ALU.mult))
                then(dve.tensor_reduce(stat[:, 1, :], key[:, :, :], AX_X, ALU.max))
                then(dve.tensor_tensor(oh1[:, :, :], key[:, :, :], wide(1), ALU.is_equal))
                then(dve.scalar_tensor_tensor(lg2[:, :, :], oh1[:, :, :], -1e30, lg[:, :, :], ALU.mult, ALU.add))
                then(dve.tensor_reduce(stat[:, 2, :], lg2[:, :, :], AX_X, ALU.max))
                then(dve.tensor_tensor(eq[:, :, :], lg2[:, :, :], wide(2), ALU.is_equal))
                then(dve.tensor_tensor(key[:, :, :], eq[:, :, :], rank, ALU.mult))
                then(dve.tensor_reduce(stat[:, 3, :], key[:, :, :], AX_X, ALU.max))
                then(dve.tensor_tensor(oh2[:, :, :], key[:, :, :], wide(3), ALU.is_equal))
                then(dve.tensor_tensor(stat[:, 4, :], stat[:, 2, :], stat[:, 0, :], ALU.subtract))
                dve.wait_ge(s["pair_exp"], i + 1)
                then(dve.tensor_scalar(stat[:, 6, :], stat[:, 5, :], 1.0, None, ALU.add))
                then(dve.reciprocal(stat[:, 6, :], stat[:, 6, :]))
                then(dve.tensor_tensor(stat[:, 7, :], stat[:, 5, :], stat[:, 6, :], ALU.mult))
                then(dve.tensor_tensor(oh1[:, :, :], oh1[:, :, :], wide(6), ALU.mult))
                then(dve.tensor_tensor(oh2[:, :, :], oh2[:, :, :], wide(7), ALU.mult))
                then(dve.tensor_tensor(comb[:, :, :], oh1[:, :, :], oh2[:, :, :], ALU.add))
                for st in range(MS):
                    p = st % 2
                    n = i * MS + st
                    dve.wait_ge(s["hid_done"], n + 1)
                    dve.wait_ge(s["bcast_ready"], n + 1)
                    if st >= 2:
                        dve.wait_ge(s["acc_done"], n - 1)
                    dve.tensor_tensor(two(gated[:, p, :]), ps[:, 6:8, 0:Q], two(hid[:, p, :]), ALU.mult)\
                        .then_inc(s["gated_ready"], 1)
                dve.wait_ge(s["acc_done"], i * MS + MS)
                dve.wait_ge(s["hx2_ready"], i + 1)
                dve.tensor_tensor(two(fin[:, :]), ps[:, 4:6, 0:Q], two(hx[:, :]), ALU.add).then_inc(s["fin_ready"], 1)

        @block.tensor
        def _(pe):
            def mm(o, lhsT, rhs, start=True, stop=True):
                return pe.matmul(o, lhsT, rhs, start=start, stop=stop, skip_group_check=True)

            pe.wait_ge(s["packed_in"], 16)
            pe.wait_ge(s["memset_done"], 10)
            mm(ps[:, 0, 0:NF + 1], mean_h[:, :], w("tok")).then_inc(s["tok_mean"], 1)
            pe.wait_ge(s["prepped"], NPREP)
            pe.wait_ge(s["prep_wait"], 2)
            pe.wait_ge(s["tokw_ready"], 1)

            def layer_norm(src):
                def part(i, k):
                    for b in range(2):
                        last = mm(ps[:, b, 0:Q], w("center"), src[:, b * Q:(b + 1) * Q])
                    last.then_inc(s["ln_centered"], 1)
                    pe.wait_ge(s["ln_squared"], i * LNS + k + 1)
                    for b in range(2):
                        last = mm(ps[:, 2 + b, 0:Q], w("avg"), ln_sq[:, b * Q:(b + 1) * Q])
                    last.then_inc(s["ln_var"], 1)
                return part

            def lo(h):
                return slice(CH * h, CH * h + CH)

            with pe.Fori(0, NBLK) as i:
                pe.wait_ge(s["tok_step"], i * 4 + 5)
                pe.wait_ge(s["outT_ready"], i + 1)
                tv = tokT[:, :, :].rearrange("p (k h) j -> p k (h j)", h=2)
                for k in range(4):
                    last = pe.transpose(ps[:, 0, k * 128:(k + 1) * 128], tv[:, k, :], w("ident"))
                last.then_inc(s["h_turned"], 1)
                pe.wait_ge(s["h_ready"], i + 1)
                layer_norm(H)(i, 0)
                pe.wait_ge(s["ln_done"], i * LNS + 1)
                layer_norm(x0)(i, 1)
                pe.wait_ge(s["ln_done"], i * LNS + 2)
                layer_norm(h1)(i, 2)
                pe.wait_ge(s["ln_done"], i * LNS + 3)
                for c, name in ((0, "xm_ready"), (1, "res_ready")):
                    for k in range(4):
                        h = k // 2
                        last = mm(ps[:, 4 * c + k, 0:Q], w("w_in")[lo(h), c * 128:(c + 1) * 128],
                                  h2[lo(h), (k % 2) * Q:(k % 2 + 1) * Q])
                    last.then_inc(s[name], 1)
                pe.wait_ge(s["xm_padded"], i + 1)
                for k in range(4):
                    for tap in range(DCONV):
                        last = mm(ps[:, k, 0:Q], diag_conv[:, tap, :], xm_pad[:, k * IQ:(k + 1) * IQ, tap:tap + L],
                                  start=(tap == 0), stop=(tap == DCONV - 1))
                last.then_inc(s["conv_ready"], 1)
                pe.wait_ge(s["u_ready"], i + 1)
                for k in range(4):
                    last = mm(ps[0:DTR, 4 + k, 0:Q], w("w_dtr"), u[:, k * Q:(k + 1) * Q])
                last.then_inc(s["dt_ready"], 1)
                pe.wait_ge(s["dts_ready"], i + 1)
                for k in range(4):
                    last = mm(ps[:, k, 0:Q], w("w_dt"), dts[:, k * Q:(k + 1) * Q])
                last.then_inc(s["v_ready"], 1)
                for g in range(NG):
                    b = 4 if g % 2 == 0 else 0
                    if g == 1:
                        pe.wait_ge(s["soft_abs"], i + 1)
                        pe.wait_ge(s["soft_relu"], i + 1)
                    if g == 2:
                        pe.wait_ge(s["bc_copied"], i * NG * 2 + 2)
                    for k in range(4):
                        last = mm(ps[0:96, b + k, 0:Q], w("w_bc")[:, g * 96:(g + 1) * 96], u[:, k * Q:(k + 1) * Q])
                    last.then_inc(s["bc_ready"], 1)
                pe.wait_ge(s["bc_copied"], i * NG * 2 + 6)
                pe.wait_ge(s["split_step"], (i + 1) * NG * 3)

                for o, t, c in pieces(Y0):
                    mm(flat[:, o:o + c], diagD[:, :], u[:, t:t + c], stop=False)

                def spread(n, g, r):
                    pe.wait_ge(s["q_done"], n + NBUF)
                    for o, t, c in pieces(B0):
                        last = mm(flat[:, o:o + c], sel[:, bass.ds(r, 1), :].rearrange("p a b -> p (a b)"),
                                  stack[:, g, t:t + c])
                    for o, t, c in pieces(C0):
                        last = mm(flat[:, o:o + c], sel[:, bass.ds(GR + r, 1), :].rearrange("p a b -> p (a b)"),
                                  stack[:, g, t:t + c])
                    last.then_inc(s["BC_ready"], 1)

                def add_up(n, p):
                    pe.wait_ge(s["z_done"], n + 1 + NBUF)
                    for o, t, c in pieces(Y0):
                        last = mm(flat[:, o:o + c], half_ident[:, :], z[:, p, t:t + c], start=False, stop=False)
                    last.then_inc(s["y_added"], 1)

                spread(i * DST, 0, 0)
                spread(i * DST + 1, 0, 1)
                for g in range(NG):
                    with pe.Fori(0, GR // 2 - 1) as j:
                        for p in range(2):
                            n = i * DST + g * GR + j * 2 + p
                            spread(n + 2, g, j * 2 + p + 2)
                            add_up(n, p)
                    for p in range(2):
                        n = i * DST + g * GR + GR - 2 + p
                        if g < NG - 1:
                            spread(n + 2, g + 1, p)
                        add_up(n, p)

                pe.wait_ge(s["yg_ready"], i + 1)
                for h in range(2):
                    for b in range(2):
                        last = mm(ps[lo(h), 3 + b, 0:Q], w_out_half[:, :], yg[:, h * TH + b * Q:h * TH + (b + 1) * Q])
                last.then_inc(s["proj_ready"], 1)
                pe.wait_ge(s["x1_ready"], i + 1)
                layer_norm(x1)(i, 3)
                pe.wait_ge(s["ln_done"], i * LNS + 4)
                for b in range(4):
                    mm(ps[0:L, b, :], ones_row[:, :], w("bn1_b"), stop=False)
                    for e in range(IQ):
                        img = b * IQ + e
                        h, t = img // HI, (img % HI) * L
                        last = mm(ps[0:L, b, e * 128:(e + 1) * 128], h3[lo(h), t:t + L], fc1s[lo(h), :], start=False)
                last.then_inc(s["f_ready"], 1)
                pe.wait_ge(s["fT_ready"], i + 1)
                F2 = 2 * NFREQ
                for img in range(BI):
                    last = mm(ps[:, 4 + img // IQ, (img % IQ) * F2:(img % IQ + 1) * F2],
                              fT[:, img * 128:(img + 1) * 128], w("dft"))
                last.then_inc(s["dft_ready"], 1)
                pe.wait_ge(s["ri_ready"], i + 1)
                for c, (wre, wim) in enumerate(((w("Wr"), negWi[:, :]), (w("Wi"), w("Wr")))):
                    for b in range(2):
                        part = ri[:, 2 * b:2 * b + 2, :].rearrange("p b (e f) -> p (b e) f", f=F2)
                        mm(ps[:, 2 * c + b, 0:8 * NFREQ], wre, part[:, :, 0:NFREQ], stop=False)
                        last = mm(ps[:, 2 * c + b, 0:8 * NFREQ], wim, part[:, :, NFREQ:F2], start=False)
                last.then_inc(s["mix_ready"], 1)
                pe.wait_ge(s["xx_ready"], i * 2 + 2)
                for img in range(BI):
                    h, e = img // HI, img % HI
                    last = mm(ps[0:F2, 4 + e // 4, (e % 4) * 128 + h * CH:(e % 4) * 128 + (h + 1) * CH],
                              xx[:, img, :], w("fc2"))
                last.then_inc(s["fc2_ready"], 1)
                pe.wait_ge(s["gmat_ready"], i + 1)
                for e in range(HI):
                    last = mm(ps[:, e // 4, (e % 4) * L:(e % 4 + 1) * L], gmat[:, e * 128:(e + 1) * 128], w("idft"))
                last.then_inc(s["ff_ready"], 1)
                pe.wait_ge(s["hA_ready"], i + 1)
                layer_norm(hA)(i, 4)
                pe.wait_ge(s["ln_done"], i * LNS + 5)
                for img in range(BI):
                    h, t = img // HI, (img % HI) * L
                    last = mm(ps[0:L, 4 + h, (img % HI) * NE:(img % HI + 1) * NE], xf[lo(h), t:t + L], w("router")[lo(h), :])
                last.then_inc(s["logits_ready"], 1)
                pe.wait_ge(s["route_step"], (i + 1) * RS)
                for img in range(BI):
                    last = pe.transpose(ps[0:NE, 4 + img // IQ, (img % IQ) * L:(img % IQ + 1) * L], comb[:, img, :],
                                        w("ident")[0:L, 0:L])
                last.then_inc(s["comb_turned"], 1)
                pe.wait_ge(s["combT_ready"], i + 1)
                for h in range(2):
                    for b in range(2):
                        mm(ps[lo(h), 4 + b, 0:Q], w("b2"), combT[:, h * TH + b * Q:h * TH + (b + 1) * Q], stop=False)

                def hidden(st):
                    k, h = st // 2, st % 2
                    if st >= 2:
                        pe.wait_ge(s["hid_done"], i * MS + st - 1)
                    for b in range(2):
                        last = mm(ps[:, 2 * (st % 2) + b, 0:Q], w("w1")[lo(h), k * 128:(k + 1) * 128],
                                  xf[lo(h), b * Q:(b + 1) * Q])
                    last.then_inc(s["hid_ready"], 1)

                def spread_weights(st):
                    k, h = st // 2, st % 2
                    if st >= 1:
                        pe.wait_ge(s["gated_ready"], i * MS + st)
                    for b in range(2):
                        last = mm(ps[:, 6 + b, 0:Q], w("pick")[:, k * 128:(k + 1) * 128],
                                  combT[:, h * TH + b * Q:h * TH + (b + 1) * Q])
                    last.then_inc(s["bcast_ready"], 1)

                hidden(0)
                spread_weights(0)
                for st in range(MS):
                    k, h = st // 2, st % 2
                    if st + 1 < MS:
                        hidden(st + 1)
                        spread_weights(st + 1)
                    pe.wait_ge(s["gated_ready"], i * MS + st + 1)
                    for b in range(2):
                        last = mm(ps[lo(h), 4 + b, 0:Q], w("w2")[:, k * CH:(k + 1) * CH],
                                  gated[:, st % 2, b * Q:(b + 1) * Q], start=False, stop=(st >= MS - 2))
                    last.then_inc(s["acc_done"], 1)
                pe.wait_ge(s["fin_ready"], i + 1)
                for e in range(HI):
                    last = pe.transpose(ps[0:L, e // 4, (e % 4) * 128:(e % 4 + 1) * 128], fin[:, e * L:(e + 1) * L],
                                        w("ident"))
                last.then_inc(s["out_turned"], 1)


def host_pack(inp):
    import numpy as np

    def twice(v):
        return np.concatenate([v, v], axis=0)

    def col(name):
        return np.reshape(inp[name], (-1, 1))

    ident = np.eye(128, dtype=np.float32)
    block_avg = np.kron(np.eye(2), np.full((CH, CH), 1.0 / CH)).astype(np.float32)
    l, f = np.arange(L)[:, None], np.arange(NFREQ)[None, :]
    ang = 2 * np.pi * ((l * f) % L) / L
    dft = np.concatenate([np.cos(ang), -np.sin(ang)], axis=1) / np.sqrt(L)
    weight = np.where(f == 0, 1.0, 2.0)
    idft = np.concatenate([weight * np.cos(ang), -weight * np.sin(ang)], axis=1).T / np.sqrt(L)
    pick = np.kron(np.eye(NE), np.ones((1, CH)))
    A = "L0_attn_"
    w_bc = inp[A + "w_xproj"]
    groups = []
    for g in range(NG):
        b = w_bc[:, DTR + g * GR:DTR + (g + 1) * GR]
        c = w_bc[:, DTR + DST + g * GR:DTR + DST + (g + 1) * GR]
        groups += [b, c] * 3
    w1 = inp["L0_ffn_w1"].reshape(4, 2, CH, CH).transpose(2, 0, 1, 3).reshape(CH, 4 * 128)
    w2 = inp["L0_ffn_w2"].reshape(4, 2, CH, CH).transpose(1, 2, 0, 3).reshape(128, 4 * CH)
    parts = dict(
        tok=np.concatenate([inp["L0_tok_W"], col("L0_tok_b")], axis=1), ident=ident, center=ident - block_avg,
        avg=block_avg, w_in=twice(inp[A + "w_in"]), conv_w=inp[A + "conv_w"].T, conv_b=col(A + "conv_b"),
        b_dt=col(A + "b_dt"), D=col(A + "D"), rb=col(A + "rb"), ib=col(A + "ib"), cls=twice(col("cls_tok")),
        b1=inp["L0_ffn_b1"].reshape(4, 128).T, A_log=inp[A + "A_log"], w_dtr=w_bc[:, 0:DTR],
        w_bc=np.concatenate(groups, axis=1), w_dt=inp[A + "w_dt"], onehot=np.tile(np.eye(32), (3, 1)),
        w_out=inp[A + "w_out"], fc1=twice(inp[A + "fc1_w"]), bn1_s=np.broadcast_to(inp[A + "bn1_s"], (128, 128)),
        bn1_b=np.tile(inp[A + "bn1_b"], 4)[None], Wr=inp[A + "Wr"], Wi=inp[A + "Wi"], fc2=inp[A + "fc2_w"],
        dft=dft, idft=idft, router=twice(inp["L0_ffn_router_w"].T), w1=twice(w1), w2=w2, b2=inp["L0_ffn_b2"],
        pick=pick, rank=np.broadcast_to(NE - np.arange(NE), (128, NE)))
    for name in ("ln1_g", "ln1_b", "mln_g", "mln_b", "ln2_g", "ln2_b", "bn2_s", "bn2_b"):
        parts[name] = twice(col(A + name))
    packed = np.zeros((128, PACK_COLS), np.float32)
    for name, (cols, rows) in PACK.items():
        packed[0:rows, PACK_AT[name]:PACK_AT[name] + cols] = parts[name]
    return packed


def kernel(**inputs):
    import numpy as _np
    import concourse.bacc as _bacc
    from concourse import mybir as _mybir
    from concourse.bass_utils import run_bass_kernel_spmd as _run

    inp = {k: _np.asarray(v) for k, v in inputs.items()}
    arrays = {"x_dram": _np.ascontiguousarray(inp["x"]), "packed_dram": host_pack(inp)}
    nc = _bacc.Bacc("TRN2", target_bir_lowering=False, num_devices=1)
    x, packed = (nc.dram_tensor(k, v.shape, _mybir.dt.from_np(v.dtype), kind="ExternalInput").ap()
                 for k, v in arrays.items())
    out = nc.dram_tensor("out_dram", (NIMG, L, CH), F32, kind="ExternalOutput").ap()
    build(nc, x, packed, out)
    r = _run(nc, [arrays], core_ids=[0])
    return r.results[0]["out_dram"]
```

```python
from contextlib import ExitStack

import concourse.bass as bass
from concourse import mybir

F32 = mybir.dt.float32
BF16 = mybir.dt.bfloat16
ALU = mybir.AluOpType
ACT = mybir.ActivationFunctionType
AX_X = mybir.AxisListType.X

NIMG, GRID, CH = 128, 64, 64
NF = 4
L = GRID + 1
DIN = 2 * CH
DTR, DST, DCONV = CH // 16, 48, 4
NE = 8
NFREQ = L // 2 + 1
BI = 16
HI = BI // 2
NBLK = NIMG // BI
T = BI * L
TH = HI * L
Q = T // 4
IQ = BI // 4
NG, GR = 3, 16
BANK = 512
TM = BI * GRID
ROOM = 7840

EARLY = """yg tail_B tail_A tail_a tail_dBu tail_C tail_ax tail_x tail_z tail_y tail_yd yg_last proj x1 hx""".split()
PRE = """tok_a tok_b turn h_out ln0_c ln0_s ln0_v ln0_r ln0_d ln1_c ln1_s ln1_v ln1_r ln1_d ln1_a
    ln2_c ln2_s ln2_v ln2_r ln2_d ln2_a xm0 xm0_out xm1 xm1_out res0 res0_t res0_g res1 res1_t res1_g
    cv0_a cv0_b cv0_t cv0_u cv1_a cv1_b cv1_t cv1_u dt0 dt0_out v0 v0_abs v0_exp v0_rnd v0_sum dt1 dt1_out v1 v1_abs
    v1_exp v1_rnd v1_sum bc0 bc0_out dsum bc1 bc1_out bc2 bc2_out bc3 bc3_out bc4 bc4_out bc5 bc5_out""".split()
LATE = """ln3_c ln3_s ln3_v ln3_r ln3_d ln3_a f0_a f0_b f0_out dft0 dft0_out mix0 mix0_out fc20 fc20_out
    f1_a f1_b f1_out dft1 dft1_out mix1 mix1_out fc21 fc21_out idft ff hA ln4_c ln4_s ln4_v ln4_r ln4_d hx2
    logits logits_out hid0 hid0_out route0 hid1 hid1_out route1 hid2 hid2_out route2 hid3 hid3_out route3 gelu0
    pair_exp route4 comb0 comb0_out comb1 comb1_out pick0 gate0 pick1 gate1 pick2 gate2 pick3 gate3 acc0_a acc0_b fin0
    hid4 hid4_out hid5 hid5_out hid6 hid6_out hid7 hid7_out gelu1
    pick4 gate4 pick5 gate5 pick6 gate6 pick7 gate7 acc1_a acc1_b fin1 out_turn out_out""".split()
FIRST_TURN, LAST_TURN = 5, 3 * DST - 6
STAGES = EARLY + PRE + LATE
TURNS = [(name, FIRST_TURN + k * (LAST_TURN - FIRST_TURN) // (len(STAGES) - 1)) for k, name in enumerate(STAGES)]
HALF_LN = 13.815510557964274

PACK = dict(
    tok=(NF + 1, 128), ident=(128, 128), center=(128, 128), avg=(128, 128), w_in=(256, 128), conv_w=(DCONV, 128),
    conv_b=(1, 128), b_dt=(1, 128), D=(1, 128), rb=(1, 128), ib=(1, 128), ln1_g=(1, 128), ln1_b=(1, 128),
    mln_g=(1, 128), mln_b=(1, 128), ln2_g=(1, 128), ln2_b=(1, 128), bn2_s=(1, 128), bn2_b=(1, 128), cls=(1, 128),
    b1=(4, 128), A_log=(DST, 128), w_dtr=(DTR, 128), w_bc=(NG * 96, 128), w_dt=(128, DTR), onehot=(32, 96),
    w_out=(CH, 128), fc1=(128, 128), bn1_s=(128, 128), bn1_b=(BANK, 1), Wr=(128, 128), Wi=(128, 128),
    fc2=(CH, 128), dft=(2 * NFREQ, L), idft=(L, 2 * NFREQ), router=(NE, 128), w1=(4 * 128, 128), w2=(4 * CH, 128),
    b2=(CH, NE), pick=(4 * 128, NE), rank=(NE, 128))
PACK_AT = {}
_at = 0
for _name, (_w, _) in PACK.items():
    PACK_AT[_name] = _at
    _at += _w
PACK_COLS = _at


def build(nc, x, packed, out):
    with ExitStack() as ctx:
        def sb(name, shape, dt=F32):
            return ctx.enter_context(nc.sbuf_tensor(name, shape, dt))

        def sem(name):
            return ctx.enter_context(nc.semaphore(name))

        pack = sb("pack", [128, PACK_COLS])

        def w(name):
            cols, rows = PACK[name]
            return pack[0:rows, PACK_AT[name]:PACK_AT[name] + cols]

        eps_col = sb("eps_col", [128, 4])
        credit = sb("credit", [128, 16])
        mean_h = sb("mean_h", [128, 128])
        tokw = sb("tokw", [128, NF + 1])
        Aneg = sb("Aneg", [128, DST])
        Ahalf = sb("Ahalf", [128, DST])
        half_ident = sb("half_ident", [128, 128])
        diagD = sb("diagD", [128, 128])
        diag_conv = sb("diag_conv", [128, DCONV, 128])
        conv_bh = sb("conv_bh", [128, 1])
        w_out_half = sb("w_out_half", [128, CH])
        fc1s = sb("fc1s", [128, 128])
        negWi = sb("negWi", [128, 128])
        sel = sb("sel", [96, 32, 128], BF16)
        ones_row = sb("ones_row", [1, L])
        not_last = sb("not_last", [128, BI, L], BF16)

        delta = sb("delta", [128, 2, T + 1])
        dsum = sb("dsum", [128, 2, T])
        du = sb("du", [128, 2, T])
        gate2 = sb("gate2", [128, 2, T])
        stack = sb("stack", [96, 2, NG, T], BF16)
        H = sb("H", [128, 2, TH])
        x0 = sb("x0", [128, 2, TH])
        u = sb("u", [128, T])
        u_last = sb("u_last", [128, 2, BI])
        a = sb("a", [128, 2, BI, GRID])
        m = sb("m", [128, 2, TM])
        q = sb("q", [128, 2, TM])
        xs = sb("xs", [128, 2, TM])
        z = sb("z", [128, 2, TM])
        x_end = sb("x_end", [128, 2, DST, BI])
        a_last = sb("a_last", [128, DST, BI])
        dBu_last = sb("dBu_last", [128, DST, BI])
        y_last = sb("y_last", [128, BI])
        yg = sb("yg", [128, T])
        x1 = sb("x1", [128, TH])
        hx = sb("hx", [128, TH])
        xin = sb("xin", [128, 4, 2, CH * NF])
        outT = sb("outT", [L, HI, 2, CH])
        ln_c = sb("ln_c", [128, TH])
        ln_sq = sb("ln_sq", [128, TH])
        ln_r = sb("ln_r", [128, TH])
        ln_y = ln_sq
        room = sb("room", [128, ROOM])
        used = {"pre": 0, "post": 0}

        def share(who, cols, rows=128):
            o = used[who]
            used[who] += cols
            assert used[who] <= ROOM, (who, used[who])
            return room[0:rows, o:o + cols]

        tokT = share("pre", 2 * 4 * CH).rearrange("p (k j) -> p k j", j=CH)
        h1 = share("pre", TH)
        h2 = share("pre", TH)
        xm_pad = share("pre", BI * (L + DCONV - 1)).rearrange("p (e l) -> p e l", e=BI)
        th = share("pre", TH)
        vh = share("pre", TH)
        dts = share("pre", TH, DTR)
        s_relu = share("pre", TH)
        s_abs = share("pre", TH)
        s_exp = share("pre", TH)
        s_log = share("pre", TH)
        pf = share("pre", 2 * TH, 64).rearrange("p (k c) -> p k c", k=2)
        rest = share("pre", TH, 64)

        h3 = share("post", TH)
        ff = share("post", TH)
        fin = ff
        hA = share("post", TH)
        xf = share("post", TH)
        combT = share("post", T, NE)
        lg, lg2, eq, key, oh1, oh2, comb = (
            share("post", BI * NE, L).rearrange("p (e x) -> p e x", x=NE) for _ in range(7))
        stat = share("post", 8 * BI, L).rearrange("p (k e) -> p k e", e=BI)
        both = used["post"]
        fT = share("post", 2 * BANK, L)
        ri = share("post", HI * 2 * NFREQ).rearrange("p (e f) -> p e f", e=HI)
        xx = share("post", HI * 2 * NFREQ).rearrange("p (e f) -> p e f", e=HI)
        gmat = share("post", 2 * BANK, 2 * NFREQ).rearrange("p (e h c) -> p e h c", e=HI, h=2)
        used["post"] = both
        hid = share("post", 4 * TH).rearrange("p (k c) -> p k c", k=4)

        ps = ctx.enter_context(nc.psum_tensor("ps", [128, 8, BANK], F32))
        psY, psB, psC, side = ps[:, 0:2, :], ps[:, 2:4, :], ps[:, 4:6, :], ps[:, 6:8, :]

        def two(t2d, c=Q):
            return t2d.rearrange("p (b c) -> p b c", c=c)

        def head(t2d):
            return t2d.rearrange("p (e l) -> p e l", l=L)[:, :, 0:GRID]

        def last_of(t2d):
            return t2d.rearrange("p (e l) -> p e l", l=L)[:, :, GRID]

        def over_n(t2d):
            return t2d.unsqueeze(1).to_broadcast([128, DST, BI])

        names = """packed_in x_in consts_set prepped mask_sel_ready tok_mean tokw_ready A_exp tok_step h_turned h_ready
            pre_centered pre_copied pre_squared pre_var pre_log pre_rstd pre_scaled pre_done
            post_centered post_copied post_squared post_var post_log post_rstd post_scaled post_done xm_ready xm_padded pads_zeroed res_ready
            res_tanh gate_ready conv_ready conv_tanh conv_half u_ready dt_ready dts_ready v_ready soft_relu soft_abs
            soft_exp soft_log soft_round soft_step du_ready dsum_ready bc_ready bc_high bc_copied split_step
            u_kept a_ready m_ready B_ready C_ready dBu_done q_done x_done z_done y_added x_kept
            yg_ready tailB_ready tailC_ready tail_A tail_a tail_dBu tail_ax tail_x tail_z tail_y tail_yd yg_last
            proj_ready x1_ready hx_ready f_ready fT_ready dft_ready ri_ready mix_ready xx_ready fc2_ready gmat_ready
            ff_ready ff_scaled hA_ready hx2_ready logits_ready route_step pair_exp comb_turned combT_ready
            hid_ready hid_copied gelu_done pick_ready gated_ready acc_ready fin_ready out_turned outT_ready
            out_stored"""
        s = {n: sem(n) for n in names.split()}
        NPREP = 12
        NBUF = 2
        LNS = {"pre": 3, "post": 2}
        AFFINE = {"pre": 2, "post": 1}
        NR = 2 * NG
        RS = 19

        x_v = x.rearrange("(n h k e) i j f -> n (e i) k h (j f)", n=NBLK, h=2, k=4)
        out_v = out.rearrange("(n h e) l c -> n h l e c", n=NBLK, h=2)

        def lo(h):
            return slice(CH * h, CH * h + CH)

        def cols(h, b=0, n=TH):
            return slice(h * TH + b * Q, h * TH + b * Q + n)

        def pre_blocks(b):
            return b + 3 if not isinstance(b, int) else min(b + 3, NBLK)

        def side_work_at(place, offset, work, i, ip, pre, post):
            for name, turn in TURNS:
                if name in work and min(max(turn + offset, 0), 3 * DST - 1) == place:
                    if name in PRE and pre:
                        work[name](i + 1, 1 - ip)
                    if name not in PRE and post:
                        work[name](i - 1, 1 - ip)

        def side_work_alone(names, work, b, p):
            for name in names:
                if name in work:
                    work[name](b, p)

        def iterations(eng, iteration):
            iteration(0, 0, True, False)
            with eng.Fori(0, NBLK // 2 - 1) as j:
                iteration(j * 2 + 1, 1, True, True)
                iteration(j * 2 + 2, 0, True, True)
            iteration(NBLK - 1, 1, False, True)

        block = ctx.enter_context(nc.Block())

        @block.sync
        def _(sp):
            sp.dma_start(pack[:, :], packed).then_inc(s["packed_in"], 16)
            sp.wait_ge(s["consts_set"], 10)

            def load(b):
                for h in range(2):
                    sp.dma_start(xin[:, :, h, :], x_v[b, :, :, h, :]).then_inc(s["x_in"], 16)

            def store(b):
                sp.wait_ge(s["outT_ready"], b + 2)
                for h in range(2):
                    sp.dma_start(out_v[b, h], outT[:, :, h, :]).then_inc(s["out_stored"], 16)

            load(0)
            sp.wait_ge(s["tok_step"], 1 + NF)
            load(1)
            sp.wait_ge(s["tok_step"], 1 + 2 * NF)
            load(2)
            with sp.Fori(0, NBLK - 3) as j:
                sp.wait_ge(s["tok_step"], j * NF + 1 + 3 * NF)
                load(j + 3)
                store(j)
            for b in range(NBLK - 3, NBLK):
                store(b)
            sp.wait_ge(s["out_stored"], 32 * NBLK + 1)

        @block.gpsimd
        def _(pool):
            for k, v in enumerate((1e-5, 1e-3, 1.0, HALF_LN)):
                pool.memset(eps_col[:, k:k + 1], v).then_inc(s["consts_set"], 1)
            pool.memset(mean_h[:, :], 1.0 / 128).then_inc(s["consts_set"], 1)
            pool.memset(ones_row[:, :], 1.0).then_inc(s["consts_set"], 1)
            for p in range(2):
                pool.memset(delta[:, p, T:T + 1], 0.0).then_inc(s["consts_set"], 1)
            pool.memset(not_last[:, :, 0:GRID], 1.0).then_inc(s["consts_set"], 1)
            pool.memset(not_last[:, :, GRID:L], 0.0).then_inc(s["consts_set"], 1)
            credits = ["tok_step", "outT_ready", "out_stored"] + ["q_done", "z_done", "y_added", "x_kept"] * NBUF
            for k, name in enumerate(credits):
                pool.memset(credit[:, k:k + 1], 0.0).then_inc(s[name], 1)
            for p in range(NBUF):
                pool.memset(a[:, p, :, 0:1], 0.0).then_inc(s["x_done"], 1)

            work = {}

            def soft_sum(h):
                def stage(b, p):
                    n = b * 2 + h
                    pool.wait_ge(s["soft_round"], n + 1)
                    pool.tensor_tensor(s_abs, s_exp, s_abs, ALU.subtract).then_inc(s["soft_step"], 1)
                    pool.wait_ge(s["soft_step"], n * 3 + 1)
                    pool.wait_ge(s["soft_log"], n + 1)
                    pool.tensor_tensor(s_log, s_abs, s_log, ALU.add).then_inc(s["soft_step"], 1)
                    pool.wait_ge(s["soft_step"], n * 3 + 2)
                    pool.tensor_tensor(delta[:, p, cols(h)], s_log, s_relu, ALU.add).then_inc(s["soft_step"], 1)
                    pool.wait_ge(s["soft_step"], n * 3 + 3)
                    pool.tensor_tensor(du[:, p, cols(h)], delta[:, p, cols(h)], u[:, cols(h)], ALU.mult)\
                        .then_inc(s["du_ready"], 1)
                return stage

            def split(r):
                g, h = r // 2, r % 2

                def stage(b, p):
                    n = b * NR + r
                    st = stack[:, p, g, cols(h)]
                    pool.wait_ge(s["bc_high"], n + 1)
                    pool.wait_ge(s["bc_copied"], n + 1)
                    if r or not isinstance(b, int) or b:
                        pool.wait_ge(s["split_step"], n * 3)
                    pool.tensor_tensor(rest, pf[:, r % 2, :], st[0:64], ALU.subtract).then_inc(s["split_step"], 1)
                    pool.wait_ge(s["split_step"], n * 3 + 1)
                    pool.tensor_tensor(st[0:64], pf[:, r % 2, :], st[0:64], ALU.subtract).then_inc(s["split_step"], 1)
                    pool.wait_ge(s["split_step"], n * 3 + 2)
                    pool.tensor_tensor(st[0:32], rest[0:32], st[0:32], ALU.subtract).then_inc(s["split_step"], 1)
                return stage

            for h in range(2):
                work[f"v{h}_sum"] = soft_sum(h)
            for r in range(NR):
                work[f"bc{r}_out"] = split(r)

            def tail_A(b, p):
                pool.wait_ge(s["soft_step"], b * 6 + 6)
                pool.tensor_tensor(a_last[:, :, :], Aneg[:, :].unsqueeze(2).to_broadcast([128, DST, BI]),
                                   over_n(last_of(delta[:, p, 0:T])), ALU.mult).then_inc(s["tail_A"], 1)

            def tail_ax(b, p):
                pool.wait_ge(s["tail_a"], b + 1)
                pool.wait_ge(s["x_kept"], (b + 1) * DST + NBUF)
                pool.tensor_tensor(a_last[:, :, :], a_last[:, :, :], x_end[:, p, :, :], ALU.mult)\
                    .then_inc(s["tail_ax"], 1)

            def tail_x(b, p):
                pool.wait_ge(s["tail_ax"], b + 1)
                pool.wait_ge(s["tail_dBu"], b + 1)
                pool.tensor_tensor(a_last[:, :, :], a_last[:, :, :], dBu_last[:, :, :], ALU.add)\
                    .then_inc(s["tail_x"], 1)

            def hx_sum(b, p):
                pool.wait_ge(s["x1_ready"], b + 1)
                pool.tensor_tensor(hx[:, :], H[:, p, :], x1[:, :], ALU.add).then_inc(s["hx_ready"], 1)

            def hx2_sum(b, p):
                pool.wait_ge(s["post_done"], b * 2 + 2)
                pool.tensor_tensor(hx[:, :], hA, xf, ALU.add).then_inc(s["hx2_ready"], 1)

            work |= dict(tail_A=tail_A, tail_ax=tail_ax, tail_x=tail_x, hx=hx_sum, hx2=hx2_sum)

            def iteration(i, ip, pre, post):
                for n in range(DST):
                    N, p = i * DST + n, n % 2
                    pool.wait_ge(s["x_done"], N + 1 + NBUF)
                    pool.wait_ge(s["q_done"], N + 1 + NBUF)
                    pool.wait_ge(s["y_added"], N + 1)
                    pool.tensor_tensor(z[:, p, :], q[:, p, :], xs[:, p, :], ALU.mult).then_inc(s["z_done"], 1)
                    for k in range(3):
                        side_work_at(3 * n + k, -4, work, i, ip, pre, post)

            side_work_alone(PRE, work, 0, 0)
            iterations(pool, iteration)
            side_work_alone(EARLY + LATE, work, NBLK - 1, 1)

        @block.scalar
        def _(act):
            act.wait_ge(s["packed_in"], 16)
            act.activation(Ahalf[:, :], w("A_log"), ACT.Exp).then_inc(s["A_exp"], 1)
            act.wait_ge(s["tok_mean"], 1)
            act.activation(tokw[:, :], ps[:, 0, 0:NF + 1], ACT.Copy).then_inc(s["tokw_ready"], 1)
            act.wait_ge(s["consts_set"], 10)
            act.wait_ge(s["prepped"], NPREP)

            work = {}

            def ln(name, k, which, idx, eps):
                def squares(b, p):
                    n = b * LNS[which] + idx + 1
                    act.wait_ge(s[which + "_centered"], n)
                    act.activation(two(ln_sq[:, :]), side[:, :, 0:Q], ACT.Square).then_inc(s[which + "_squared"], 1)
                    act.activation(two(ln_c[:, :]), side[:, :, 0:Q], ACT.Copy).then_inc(s[which + "_copied"], 1)

                def inverse(b, p):
                    n = b * LNS[which] + idx + 1
                    act.wait_ge(s[which + "_var"], n)
                    act.activation(two(ln_r[:, :]), side[:, :, 0:Q], ACT.Ln, bias=eps_col[:, eps:eps + 1])\
                        .then_inc(s[which + "_log"], 1)
                    act.wait_ge(s[which + "_log"], n)
                    act.activation(ln_r[:, :], ln_r[:, :], ACT.Exp, scale=-0.5).then_inc(s[which + "_rstd"], 1)

                work[name + "_s"], work[name + "_r"] = squares, inverse

            for k in range(3):
                ln(f"ln{k}", k, "pre", k, 0 if k == 0 else 1)
            ln("ln3", 3, "post", 0, 1)
            ln("ln4", 4, "post", 1, 0)

            def h_out(b, p):
                act.wait_ge(s["h_turned"], b + 1)
                if not isinstance(b, int) or b >= 2:
                    act.wait_ge(s["hx_ready"], b - 1)
                act.activation(H[:, p, :].rearrange("p (e l) -> p e l", l=L)[:, :, 1:L],
                               side[:, 0, :].rearrange("p (e l) -> p e l", l=GRID), ACT.Copy).then_inc(s["h_ready"], 1)

            work["h_out"] = h_out

            def half_stages(h):
                def xm_out(b, p):
                    act.wait_ge(s["xm_ready"], b * 2 + h + 1)
                    act.activation(xm_pad[:, h * HI:(h + 1) * HI, DCONV - 1:].rearrange("p (k e) l -> p k e l", e=IQ),
                                   side[:, :, 0:Q].rearrange("p k (e l) -> p k e l", l=L), ACT.Copy)\
                        .then_inc(s["xm_padded"], 1)

                def res_t(b, p):
                    act.wait_ge(s["res_ready"], b * 2 + h + 1)
                    if h:
                        act.wait_ge(s["gate_ready"], b * 2 + 1)
                    act.activation(two(th), side[:, :, 0:Q], ACT.Tanh, scale=0.5).then_inc(s["res_tanh"], 1)

                def cv_t(b, p):
                    act.wait_ge(s["conv_ready"], b * 2 + h + 1)
                    if h:
                        act.wait_ge(s["u_ready"], b * 2 + 1)
                    act.activation(two(vh), side[:, :, 0:Q], ACT.Identity, bias=conv_bh[:, :], scale=0.5)\
                        .then_inc(s["conv_half"], 1)
                    act.wait_ge(s["gate_ready"], b * 2 + 2)
                    act.activation(two(th), side[:, :, 0:Q], ACT.Tanh, bias=conv_bh[:, :], scale=0.5)\
                        .then_inc(s["conv_tanh"], 1)

                def dt_out(b, p):
                    act.wait_ge(s["dt_ready"], b * 2 + h + 1)
                    act.activation(two(dts), side[0:DTR, :, 0:Q], ACT.Copy).then_inc(s["dts_ready"], 1)

                def v_abs(b, p):
                    act.wait_ge(s["v_ready"], b * 2 + h + 1)
                    if h:
                        act.wait_ge(s["soft_step"], b * 6 + 3)
                    act.activation(two(s_abs), side[:, :, 0:Q], ACT.Abs, bias=w("b_dt")).then_inc(s["soft_abs"], 1)
                    act.activation(two(s_relu), side[:, :, 0:Q], ACT.Relu, bias=w("b_dt")).then_inc(s["soft_relu"], 1)

                def v_exp(b, p):
                    act.wait_ge(s["soft_abs"], b * 2 + h + 1)
                    act.activation(s_exp, s_abs, ACT.Exp, scale=-1.0).then_inc(s["soft_exp"], 1)
                    act.wait_ge(s["soft_exp"], b * 2 + h + 1)
                    act.activation(s_log, s_exp, ACT.Ln, bias=eps_col[:, 2:3]).then_inc(s["soft_log"], 1)

                def f_out(b, p):
                    act.wait_ge(s["f_ready"], b * 2 + h + 1)
                    if h:
                        act.wait_ge(s["dft_ready"], b * 2 + 1)
                    act.activation(two(fT, BANK), side[0:L, :, :], ACT.Relu).then_inc(s["fT_ready"], 1)

                def dft_out(b, p):
                    act.wait_ge(s["dft_ready"], b * 2 + h + 1)
                    act.activation(ri.rearrange("p (b e) f -> p b (e f)", b=2), side[:, :, 0:4 * 2 * NFREQ], ACT.Copy)\
                        .then_inc(s["ri_ready"], 1)

                def mix_out(b, p):
                    act.wait_ge(s["mix_ready"], b * 2 + h + 1)
                    for c, bias in ((0, "rb"), (1, "ib")):
                        act.activation(xx[:, :, c * NFREQ:(c + 1) * NFREQ],
                                       side[:, c, 0:HI * NFREQ].rearrange("p (e f) -> p e f", f=NFREQ),
                                       ACT.Relu, bias=w(bias)).then_inc(s["xx_ready"], 1)

                def fc2_out(b, p):
                    act.wait_ge(s["fc2_ready"], b * 2 + h + 1)
                    act.activation(gmat[:, :, h, :], side[0:2 * NFREQ, 0, :].rearrange("p (e c) -> p e c", c=CH),
                                   ACT.Copy).then_inc(s["gmat_ready"], 1)

                def gelu(b, p):
                    act.wait_ge(s["hid_copied"], b * 8 + 4 * h + 4)
                    act.activation(hid[:, :, :], hid[:, :, :], ACT.Gelu).then_inc(s["gelu_done"], 1)

                def comb_out(b, p):
                    act.wait_ge(s["comb_turned"], b * 2 + h + 1)
                    act.activation(two(combT[:, cols(h)]), side[0:NE, :, 0:Q], ACT.Copy).then_inc(s["combT_ready"], 1)

                work.update({f"xm{h}_out": xm_out, f"res{h}_t": res_t, f"cv{h}_t": cv_t, f"dt{h}_out": dt_out,
                             f"v{h}_abs": v_abs, f"v{h}_exp": v_exp, f"f{h}_out": f_out, f"dft{h}_out": dft_out,
                             f"mix{h}_out": mix_out, f"fc2{h}_out": fc2_out, f"gelu{h}": gelu,
                             f"comb{h}_out": comb_out})

            for h in range(2):
                half_stages(h)

            def bc_out(r):
                g, h = r // 2, r % 2

                def stage(b, p):
                    n = b * NR + r
                    act.wait_ge(s["bc_ready"], n + 1)
                    act.activation(two(stack[:, p, g, cols(h)]), side[0:96, :, 0:Q], ACT.Copy)\
                        .then_inc(s["bc_high"], 1)
                    if r >= 2:
                        act.wait_ge(s["split_step"], (n - 2) * 3 + 2)
                    act.activation(two(pf[:, r % 2, :]), side[0:64, :, 0:Q], ACT.Copy).then_inc(s["bc_copied"], 1)
                return stage

            def hid_out(r):
                def stage(b, p):
                    act.wait_ge(s["hid_ready"], b * 8 + r + 1)
                    if r >= 4:
                        act.wait_ge(s["acc_ready"], b * 2 + 1)
                    act.activation(two(hid[:, r % 4, :]), side[:, :, 0:Q], ACT.Identity,
                                   bias=w("b1")[:, r % 4:r % 4 + 1]).then_inc(s["hid_copied"], 1)
                return stage

            for r in range(NR):
                work[f"bc{r}_out"] = bc_out(r)
            for r in range(8):
                work[f"hid{r}_out"] = hid_out(r)

            def tail_a(b, p):
                act.wait_ge(s["tail_A"], b + 1)
                act.activation(a_last[:, :, :], a_last[:, :, :], ACT.Exp).then_inc(s["tail_a"], 1)

            def pair_exp(b, p):
                act.wait_ge(s["route_step"], b * RS + 13)
                act.activation(stat[:, 5, :], stat[:, 4, :], ACT.Exp).then_inc(s["pair_exp"], 1)

            def out_out(b, p):
                act.wait_ge(s["out_turned"], b + 1)
                act.wait_ge(s["out_stored"], b * 32 + 1)
                act.activation(outT[:, :, :, :].rearrange("p (b e) h c -> p b (e h c)", b=2), side[0:L, :, :],
                               ACT.Copy).then_inc(s["outT_ready"], 1)

            work |= dict(tail_a=tail_a, pair_exp=pair_exp, out_out=out_out)

            def keep_end(N, n, p):
                act.activation(x_end[:, p, n, :], xs[:, n % 2, GRID - 1::GRID], ACT.Copy).then_inc(s["x_kept"], 1)

            def iteration(i, ip, pre, post):
                first = isinstance(i, int) and i == 0
                act.wait_ge(s["u_ready"], i * 2 + 2)
                act.activation(u_last[:, ip, :], last_of(u[:, :]), ACT.Copy).then_inc(s["u_kept"], 1)
                act.wait_ge(s["soft_step"], i * 6 + 6)
                act.wait_ge(s["dsum_ready"], i + 1)
                dv = delta[:, ip, 0:T].rearrange("p (e l) -> p e l", l=L)
                for n in range(DST):
                    N, p = i * DST + n, n % 2
                    side_work_at(3 * n, 4, work, i, ip, pre, post)
                    act.wait_ge(s["x_done"], N + 1)
                    if n >= 2:
                        keep_end(N - 2, n - 2, ip)
                    elif not first:
                        keep_end(N - 2, DST + n - 2, 1 - ip)
                    act.activation(a[:, p, :, 1:GRID], dv[:, :, 1:GRID], ACT.Exp, scale=Aneg[:, n:n + 1])\
                        .then_inc(s["a_ready"], 1)
                    side_work_at(3 * n + 1, 4, work, i, ip, pre, post)
                    act.wait_ge(s["q_done"], N + 1)
                    act.activation(m[:, p, :].rearrange("p (e l) -> p e l", l=GRID), head(dsum[:, ip, :]), ACT.Tanh,
                                   scale=Ahalf[:, n:n + 1], bias=eps_col[:, 3:4]).then_inc(s["m_ready"], 1)
                    side_work_at(3 * n + 2, 4, work, i, ip, pre, post)

            side_work_alone(PRE, work, 0, 0)
            iterations(act, iteration)
            for n in (DST - 2, DST - 1):
                N = (NBLK - 1) * DST + n
                act.wait_ge(s["x_done"], N + 1 + NBUF)
                keep_end(N, n, 1)
            side_work_alone(EARLY + LATE, work, NBLK - 1, 1)

        @block.vector
        def _(dve):
            dve.wait_ge(s["packed_in"], 16)
            dve.wait_ge(s["A_exp"], 1)
            dve.tensor_scalar(Aneg[:, :], Ahalf[:, :], -1.0, None, ALU.mult).then_inc(s["prepped"], 1)
            dve.wait_ge(s["prepped"], 1)
            dve.tensor_scalar(Ahalf[:, :], Aneg[:, :], 0.5, None, ALU.mult).then_inc(s["prepped"], 1)
            dve.tensor_scalar(half_ident[:, :], w("ident"), 0.5, None, ALU.mult).then_inc(s["prepped"], 1)
            dve.tensor_scalar(diagD[:, :], w("ident"), w("D"), None, ALU.mult).then_inc(s["prepped"], 1)
            for k in range(DCONV):
                dve.tensor_scalar(diag_conv[:, k, :], w("ident"), w("conv_w")[:, k:k + 1], None, ALU.mult)\
                    .then_inc(s["prepped"], 1)
            dve.tensor_scalar(conv_bh[:, :], w("conv_b"), 0.5, None, ALU.mult).then_inc(s["prepped"], 1)
            dve.tensor_scalar(w_out_half[:, :], w("w_out"), 0.5, None, ALU.mult).then_inc(s["prepped"], 1)
            dve.tensor_tensor(fc1s[:, :], w("fc1"), w("bn1_s"), ALU.mult).then_inc(s["prepped"], 1)
            dve.tensor_scalar(negWi[:, :], w("Wi"), -1.0, None, ALU.mult).then_inc(s["prepped"], 1)
            for p in range(2):
                dve.tensor_copy(H[:, p, :].rearrange("p (e l) -> p e l", l=L)[:, :, 0:1],
                                w("cls").unsqueeze(2).to_broadcast([128, HI, 1])).then_inc(s["mask_sel_ready"], 1)
            dve.tensor_copy(sel[:, :, :], w("onehot").unsqueeze(2).to_broadcast([96, 32, 128]))\
                .then_inc(s["mask_sel_ready"], 1)
            dve.wait_ge(s["tokw_ready"], 1)
            dve.wait_ge(s["consts_set"], 10)

            work = {}
            xv = xin[:, :, :, :].rearrange("p k h (j f) -> p (k h) j f", f=NF)

            def tok(f):
                def stage(b, p):
                    if f == 0:
                        dve.wait_ge(s["x_in"], b * 32 + 32)
                        if not isinstance(b, int) or b >= 2:
                            dve.wait_ge(s["outT_ready"], b - 1)
                            dve.wait_ge(s["split_step"], b * NR * 3)
                        dve.tensor_scalar(tokT, xv[:, :, :, 0], tokw[:, 0:1], tokw[:, NF:NF + 1], ALU.mult, ALU.add)\
                            .then_inc(s["tok_step"], 1)
                        return
                    dve.wait_ge(s["tok_step"], b * NF + f + 1)
                    dve.scalar_tensor_tensor(tokT, xv[:, :, :, f], tokw[:, f:f + 1], tokT, ALU.mult, ALU.add)\
                        .then_inc(s["tok_step"], 1)
                return stage

            def tok_a(b, p):
                tok(0)(b, p)
                tok(1)(b, p)

            def tok_b(b, p):
                dve.memset(xm_pad[:, :, 0:DCONV - 1], 0.0).then_inc(s["pads_zeroed"], 1)
                tok(2)(b, p)
                tok(3)(b, p)

            def ln(name, which, idx, dst, g=None, beta=None, affine=0):
                def scale(b, p):
                    out = dst(p)
                    n = b * LNS[which] + idx + 1
                    dve.wait_ge(s[which + "_rstd"], n)
                    dve.wait_ge(s[which + "_copied"], n)
                    if g is None:
                        dve.tensor_tensor(out, ln_c[:, :], ln_r[:, :], ALU.mult).then_inc(s[which + "_done"], 1)
                        return
                    dve.scalar_tensor_tensor(ln_y[:, :], ln_c[:, :], w(g), ln_r[:, :], ALU.mult, ALU.mult)\
                        .then_inc(s[which + "_scaled"], 1)

                def shift(b, p):
                    dve.wait_ge(s[which + "_scaled"], b * AFFINE[which] + affine + 1)
                    dve.tensor_scalar(dst(p), ln_y[:, :], w(beta), None, ALU.add).then_inc(s[which + "_done"], 1)

                work[name + "_d"] = scale
                if g is not None:
                    work[name + "_a"] = shift

            ln("ln0", "pre", 0, lambda p: x0[:, p, :])
            ln("ln1", "pre", 1, lambda p: h1, "ln1_g", "ln1_b", 0)
            ln("ln2", "pre", 2, lambda p: h2, "mln_g", "mln_b", 1)
            ln("ln3", "post", 0, lambda p: h3, "ln2_g", "ln2_b", 0)
            ln("ln4", "post", 1, lambda p: xf)

            def half_stages(h):
                def res_g(b, p):
                    dve.wait_ge(s["res_tanh"], b * 2 + h + 1)
                    dve.scalar_tensor_tensor(two(gate2[:, p, cols(h)]), two(th), 1.0, side[:, :, 0:Q],
                                             ALU.add, ALU.mult).then_inc(s["gate_ready"], 1)

                def cv_u(b, p):
                    dve.wait_ge(s["conv_tanh"], b * 2 + h + 1)
                    dve.wait_ge(s["conv_half"], b * 2 + h + 1)
                    if not isinstance(b, int) or b >= 1:
                        dve.wait_ge(s["u_kept"], b)
                        dve.wait_ge(s["y_added"], (b - 1) * DST + NBUF + 1)
                    dve.scalar_tensor_tensor(u[:, cols(h)], th, 1.0, vh, ALU.add, ALU.mult).then_inc(s["u_ready"], 1)

                def v_rnd(b, p):
                    dve.wait_ge(s["soft_exp"], b * 2 + h + 1)
                    dve.tensor_scalar(s_abs, s_exp, 1.0, -1.0, ALU.add, ALU.add).then_inc(s["soft_round"], 1)

                def fin_sum(b, p):
                    dve.wait_ge(s["acc_ready"], b * 2 + h + 1)
                    dve.wait_ge(s["hx2_ready"], b + 1)
                    dve.tensor_tensor(two(fin[lo(h), :]), side[lo(h), :, 0:Q], two(hx[lo(h), :]), ALU.add)\
                        .then_inc(s["fin_ready"], 1)

                work.update({f"res{h}_g": res_g, f"cv{h}_u": cv_u, f"v{h}_rnd": v_rnd, f"fin{h}": fin_sum})

            for h in range(2):
                half_stages(h)

            def gate(r):
                def stage(b, p):
                    dve.wait_ge(s["gelu_done"], b * 2 + r // 4 + 1)
                    dve.wait_ge(s["pick_ready"], b * 8 + r + 1)
                    dve.tensor_tensor(two(hid[:, r % 4, :]), side[:, :, 0:Q], two(hid[:, r % 4, :]), ALU.mult)\
                        .then_inc(s["gated_ready"], 1)
                return stage

            for r in range(8):
                work[f"gate{r}"] = gate(r)

            def dsum_scan(b, p):
                dve.wait_ge(s["soft_step"], b * 6 + 6)
                keep = not_last[:, :, :].rearrange("p e l -> p (e l)")
                dve.tensor_tensor_scan(dsum[:, p, ::-1], delta[:, p, T:0:-1], keep[:, ::-1], 0.0, ALU.add, ALU.mult)\
                    .then_inc(s["dsum_ready"], 1)

            def yg_main(b, p):
                dve.wait_ge(s["y_added"], (b + 1) * DST + NBUF)
                dve.tensor_tensor(head(yg[:, :]), psY.rearrange("p b (e l) -> p (b e) l", l=GRID),
                                  head(gate2[:, p, :]), ALU.mult).then_inc(s["yg_ready"], 1)

            halves = side[:, :, 0:DST // 2 * BI].rearrange("p k (n e) -> p k n e", e=BI)

            def tail_dBu(b, p):
                dve.wait_ge(s["tailB_ready"], b + 1)
                dve.wait_ge(s["du_ready"], b * 2 + 2)
                dve.tensor_tensor(dBu_last[:, :, :].rearrange("p (k n) e -> p k n e", k=2), halves,
                                  last_of(du[:, p, :]).unsqueeze(1).unsqueeze(1).to_broadcast([128, 2, DST // 2, BI]),
                                  ALU.mult).then_inc(s["tail_dBu"], 1)

            def tail_z(b, p):
                dve.wait_ge(s["tailC_ready"], b + 1)
                dve.wait_ge(s["tail_x"], b + 1)
                dve.tensor_tensor(dBu_last[:, :, :].rearrange("p (k n) e -> p k n e", k=2), halves,
                                  a_last[:, :, :].rearrange("p (k n) e -> p k n e", k=2), ALU.mult)\
                    .then_inc(s["tail_z"], 1)

            def tail_y(b, p):
                dve.wait_ge(s["tail_z"], b + 1)
                dve.tensor_reduce(y_last[:, :], dBu_last[:, :, :].rearrange("p n e -> p e n"), AX_X, ALU.add)\
                    .then_inc(s["tail_y"], 1)

            def tail_yd(b, p):
                dve.wait_ge(s["tail_y"], b + 1)
                dve.wait_ge(s["u_kept"], b + 1)
                dve.scalar_tensor_tensor(y_last[:, :], u_last[:, p, :], w("D"), y_last[:, :], ALU.mult, ALU.add)\
                    .then_inc(s["tail_yd"], 1)

            def yg_end(b, p):
                dve.wait_ge(s["tail_yd"], b + 1)
                dve.tensor_tensor(last_of(yg[:, :]), y_last[:, :], last_of(gate2[:, p, :]), ALU.mult)\
                    .then_inc(s["yg_last"], 1)

            def x1_sum(b, p):
                dve.wait_ge(s["proj_ready"], b + 1)
                dve.tensor_tensor(two(x1[:, :]), side[:, :, 0:Q], two(x0[:, p, :]), ALU.add).then_inc(s["x1_ready"], 1)

            def ff_scale(b, p):
                dve.wait_ge(s["ff_ready"], b + 1)
                dve.tensor_scalar(two(ff), side[:, :, 0:Q], w("bn2_s"), w("bn2_b"), ALU.mult, ALU.add)\
                    .then_inc(s["ff_scaled"], 1)

            def hA_sum(b, p):
                dve.wait_ge(s["ff_scaled"], b + 1)
                dve.wait_ge(s["hx_ready"], b + 1)
                dve.tensor_tensor(hA, ff, hx[:, :], ALU.add).then_inc(s["hA_ready"], 1)

            def wide(k):
                return stat[:, k, :].unsqueeze(2).to_broadcast([L, BI, NE])

            rank = w("rank")[0:L, :].unsqueeze(1).to_broadcast([L, BI, NE])

            def then(b, step, ins):
                ins.then_inc(s["route_step"], 1)
                dve.wait_ge(s["route_step"], b * RS + step)

            def logits_out(b, p):
                dve.wait_ge(s["logits_ready"], b + 1)
                then(b, 1, dve.tensor_copy(lg.rearrange("p (h e) x -> p h (e x)", h=2), side[0:L, :, 0:HI * NE]))

            def route0(b, p):
                then(b, 2, dve.tensor_reduce(stat[:, 0, :], lg, AX_X, ALU.max))
                then(b, 3, dve.tensor_tensor(eq, lg, wide(0), ALU.is_equal))
                then(b, 4, dve.tensor_tensor(key, eq, rank, ALU.mult))

            def route1(b, p):
                then(b, 5, dve.tensor_reduce(stat[:, 1, :], key, AX_X, ALU.max))
                then(b, 6, dve.tensor_tensor(oh1, key, wide(1), ALU.is_equal))
                then(b, 7, dve.scalar_tensor_tensor(lg2, oh1, -1e30, lg, ALU.mult, ALU.add))

            def route2(b, p):
                then(b, 8, dve.tensor_reduce(stat[:, 2, :], lg2, AX_X, ALU.max))
                then(b, 9, dve.tensor_tensor(eq, lg2, wide(2), ALU.is_equal))
                then(b, 10, dve.tensor_tensor(key, eq, rank, ALU.mult))

            def route3(b, p):
                then(b, 11, dve.tensor_reduce(stat[:, 3, :], key, AX_X, ALU.max))
                then(b, 12, dve.tensor_tensor(oh2, key, wide(3), ALU.is_equal))
                then(b, 13, dve.tensor_tensor(stat[:, 4, :], stat[:, 2, :], stat[:, 0, :], ALU.subtract))

            def route4(b, p):
                dve.wait_ge(s["pair_exp"], b + 1)
                then(b, 14, dve.tensor_scalar(stat[:, 6, :], stat[:, 5, :], 1.0, None, ALU.add))
                then(b, 15, dve.reciprocal(stat[:, 6, :], stat[:, 6, :]))
                then(b, 16, dve.tensor_tensor(stat[:, 7, :], stat[:, 5, :], stat[:, 6, :], ALU.mult))
                then(b, 17, dve.tensor_tensor(oh1, oh1, wide(6), ALU.mult))
                then(b, 18, dve.tensor_tensor(oh2, oh2, wide(7), ALU.mult))
                then(b, 19, dve.tensor_tensor(comb, oh1, oh2, ALU.add))

            work |= dict(tok_a=tok_a, tok_b=tok_b, dsum=dsum_scan, yg=yg_main, tail_dBu=tail_dBu, tail_z=tail_z,
                         tail_y=tail_y, tail_yd=tail_yd, yg_last=yg_end, x1=x1_sum, ff=ff_scale, hA=hA_sum,
                         logits_out=logits_out, route0=route0, route1=route1, route2=route2, route3=route3,
                         route4=route4)

            def iteration(i, ip, pre, post):
                dve.wait_ge(s["du_ready"], i * 2 + 2)
                for n in range(DST):
                    N, p = i * DST + n, n % 2
                    dve.wait_ge(s["B_ready"], N + 1)
                    dve.wait_ge(s["z_done"], N + 1)
                    dve.wait_ge(s["x_kept"], N + 1)
                    dve.tensor_tensor(xs[:, p, :].rearrange("p (e l) -> p e l", l=GRID),
                                      psB.rearrange("p b (e l) -> p (b e) l", l=GRID), head(du[:, ip, :]), ALU.mult)\
                        .then_inc(s["dBu_done"], 1)
                    side_work_at(3 * n, 0, work, i, ip, pre, post)
                    dve.wait_ge(s["m_ready"], N + 1)
                    dve.wait_ge(s["C_ready"], N + 1)
                    dve.scalar_tensor_tensor(q[:, p, :], m[:, p, :], 1.0, psC.rearrange("p b c -> p (b c)"),
                                             ALU.add, ALU.mult).then_inc(s["q_done"], 1)
                    side_work_at(3 * n + 1, 0, work, i, ip, pre, post)
                    dve.wait_ge(s["a_ready"], N + 1)
                    dve.wait_ge(s["dBu_done"], N + 1)
                    dve.tensor_tensor_scan(xs[:, p, :], a[:, p, :, :].rearrange("p e l -> p (e l)"), xs[:, p, :], 0.0,
                                           ALU.mult, ALU.add).then_inc(s["x_done"], 1)
                    side_work_at(3 * n + 2, 0, work, i, ip, pre, post)

            side_work_alone(PRE, work, 0, 0)
            iterations(dve, iteration)
            side_work_alone(EARLY + LATE, work, NBLK - 1, 1)

        @block.tensor
        def _(pe):
            def mm(o, lhsT, rhs, start=True, stop=True):
                return pe.matmul(o, lhsT, rhs, start=start, stop=stop, skip_group_check=True)

            pe.wait_ge(s["packed_in"], 16)
            pe.wait_ge(s["consts_set"], 10)
            mm(ps[:, 0, 0:NF + 1], mean_h[:, :], w("tok")).then_inc(s["tok_mean"], 1)
            pe.wait_ge(s["prepped"], NPREP)
            pe.wait_ge(s["mask_sel_ready"], 3)
            pe.wait_ge(s["tokw_ready"], 1)

            work = {}
            F2 = 2 * NFREQ

            def turn(b, p):
                pe.wait_ge(s["tok_step"], b * NF + 1 + NF)
                if not isinstance(b, int) or b >= 1:
                    pe.wait_ge(s["bc_copied"], b * NR)
                if not isinstance(b, int) or b >= 2:
                    pe.wait_ge(s["x1_ready"], b - 1)
                tv = tokT.rearrange("p (k h) j -> p k (h j)", h=2)
                for k in range(4):
                    last = pe.transpose(side[:, 0, k * 128:(k + 1) * 128], tv[:, k, :], w("ident"))
                last.then_inc(s["h_turned"], 1)

            def ln(name, which, idx, src, ready):
                def center(b, p):
                    ready(b)
                    for c in range(2):
                        last = mm(side[:, c, 0:Q], w("center"), src(p)[:, c * Q:(c + 1) * Q])
                    last.then_inc(s[which + "_centered"], 1)

                def variance(b, p):
                    n = b * LNS[which] + idx + 1
                    pe.wait_ge(s[which + "_squared"], n)
                    pe.wait_ge(s[which + "_copied"], n)
                    for c in range(2):
                        last = mm(side[:, c, 0:Q], w("avg"), ln_sq[:, c * Q:(c + 1) * Q])
                    last.then_inc(s[which + "_var"], 1)

                work[name + "_c"], work[name + "_v"] = center, variance

            def after_pre(b):
                pe.wait_ge(s["bc_copied"], pre_blocks(b) * NR)
                pe.wait_ge(s["split_step"], pre_blocks(b) * NR * 3)
                pe.wait_ge(s["x1_ready"], b + 1)

            ln("ln0", "pre", 0, lambda p: H[:, p, :], lambda b: pe.wait_ge(s["h_ready"], b + 1))
            ln("ln1", "pre", 1, lambda p: x0[:, p, :], lambda b: pe.wait_ge(s["pre_done"], b * 3 + 1))
            ln("ln2", "pre", 2, lambda p: h1, lambda b: pe.wait_ge(s["pre_done"], b * 3 + 2))
            ln("ln3", "post", 0, lambda p: x1[:, :], after_pre)
            ln("ln4", "post", 1, lambda p: hA, lambda b: pe.wait_ge(s["hA_ready"], b + 1))

            def half_stages(h):
                def project(c, name, before):
                    def stage(b, p):
                        before(b)
                        for k in range(2):
                            last = mm(side[:, k, 0:Q], w("w_in")[lo(h), c * 128:(c + 1) * 128],
                                      h2[lo(h), k * Q:(k + 1) * Q])
                        last.then_inc(s[name], 1)
                    return stage

                def before_xm(b):
                    if h:
                        pe.wait_ge(s["xm_padded"], b * 2 + 1)
                    else:
                        pe.wait_ge(s["pre_done"], b * 3 + 3)

                def before_res(b):
                    if h:
                        pe.wait_ge(s["gate_ready"], b * 2 + 1)
                    else:
                        pe.wait_ge(s["xm_padded"], b * 2 + 2)

                def conv(k):
                    def stage(b, p):
                        if k == 0 and h == 0:
                            pe.wait_ge(s["gate_ready"], b * 2 + 2)
                            pe.wait_ge(s["pads_zeroed"], b + 1)
                        if k == 0 and h == 1:
                            pe.wait_ge(s["conv_tanh"], b * 2 + 1)
                        e = h * HI + k * IQ
                        for tap in range(DCONV):
                            last = mm(side[:, k, 0:Q], diag_conv[:, tap, :], xm_pad[:, e:e + IQ, tap:tap + L],
                                      start=(tap == 0), stop=(tap == DCONV - 1))
                        if k == 1:
                            last.then_inc(s["conv_ready"], 1)
                    return stage

                def dt(b, p):
                    pe.wait_ge(s["u_ready"], b * 2 + 2)
                    if h:
                        pe.wait_ge(s["soft_abs"], b * 2 + 1)
                        pe.wait_ge(s["soft_relu"], b * 2 + 1)
                    for k in range(2):
                        last = mm(side[0:DTR, k, 0:Q], w("w_dtr"), u[:, cols(h, k, Q)])
                    last.then_inc(s["dt_ready"], 1)

                def v(b, p):
                    pe.wait_ge(s["dts_ready"], b * 2 + h + 1)
                    for k in range(2):
                        last = mm(side[:, k, 0:Q], w("w_dt"), dts[:, k * Q:(k + 1) * Q])
                    last.then_inc(s["v_ready"], 1)

                def spectral_in(k):
                    def stage(b, p):
                        if k == 0 and h == 0:
                            pe.wait_ge(s["post_done"], b * 2 + 1)
                        if k == 0 and h == 1:
                            pe.wait_ge(s["gmat_ready"], b * 2 + 1)
                        mm(side[0:L, k, :], ones_row[:, :], w("bn1_b"), stop=False)
                        for e in range(IQ):
                            t = (k * IQ + e) * L
                            last = mm(side[0:L, k, e * 128:(e + 1) * 128], h3[lo(h), t:t + L], fc1s[lo(h), :],
                                      start=False)
                        if k == 1:
                            last.then_inc(s["f_ready"], 1)
                    return stage

                def dft(b, p):
                    pe.wait_ge(s["fT_ready"], b * 2 + h + 1)
                    for e in range(HI):
                        last = mm(side[:, e // IQ, (e % IQ) * F2:(e % IQ + 1) * F2], fT[:, e * 128:(e + 1) * 128],
                                  w("dft"))
                    last.then_inc(s["dft_ready"], 1)

                def mix(b, p):
                    pe.wait_ge(s["ri_ready"], b * 2 + h + 1)
                    for c, (wre, wim) in enumerate(((w("Wr"), negWi[:, :]), (w("Wi"), w("Wr")))):
                        mm(side[:, c, 0:HI * NFREQ], wre, ri[:, :, 0:NFREQ], stop=False)
                        last = mm(side[:, c, 0:HI * NFREQ], wim, ri[:, :, NFREQ:F2], start=False)
                    last.then_inc(s["mix_ready"], 1)

                def fc2(b, p):
                    pe.wait_ge(s["xx_ready"], b * 4 + 2 * h + 2)
                    for e in range(HI):
                        last = mm(side[0:F2, 0, e * CH:(e + 1) * CH], xx[:, e, :], w("fc2"))
                    last.then_inc(s["fc2_ready"], 1)

                def comb_turn(b, p):
                    if h:
                        pe.wait_ge(s["combT_ready"], b * 2 + 1)
                    else:
                        pe.wait_ge(s["route_step"], (b + 1) * RS)
                        pe.wait_ge(s["hid_copied"], b * 8 + 4)
                    for e in range(HI):
                        last = pe.transpose(side[0:NE, e // IQ, (e % IQ) * L:(e % IQ + 1) * L], comb[:, h * HI + e, :],
                                            w("ident")[0:L, 0:L])
                    last.then_inc(s["comb_turned"], 1)

                def accumulate(c):
                    def stage(b, p):
                        if c == 0:
                            pe.wait_ge(s["gated_ready"], b * 8 + 4 * h + 4)
                        mm(side[lo(h), c, 0:Q], w("b2"), combT[:, cols(h, c, Q)], stop=False)
                        for k in range(4):
                            last = mm(side[lo(h), c, 0:Q], w("w2")[:, k * CH:(k + 1) * CH],
                                      hid[:, k, c * Q:(c + 1) * Q], start=False, stop=(k == 3))
                        if c == 1:
                            last.then_inc(s["acc_ready"], 1)
                    return stage

                work.update({f"xm{h}": project(0, "xm_ready", before_xm), f"res{h}": project(1, "res_ready", before_res),
                             f"cv{h}_a": conv(0), f"cv{h}_b": conv(1), f"dt{h}": dt, f"v{h}": v,
                             f"f{h}_a": spectral_in(0), f"f{h}_b": spectral_in(1), f"dft{h}": dft, f"mix{h}": mix,
                             f"fc2{h}": fc2, f"comb{h}": comb_turn, f"acc{h}_a": accumulate(0),
                             f"acc{h}_b": accumulate(1)})

            for h in range(2):
                half_stages(h)

            def bc(r):
                g, h = r // 2, r % 2

                def stage(b, p):
                    if r == 0:
                        pe.wait_ge(s["soft_abs"], b * 2 + 2)
                        pe.wait_ge(s["soft_relu"], b * 2 + 2)
                    else:
                        pe.wait_ge(s["bc_high"], b * NR + r)
                        pe.wait_ge(s["bc_copied"], b * NR + r)
                    for k in range(2):
                        last = mm(side[0:96, k, 0:Q], w("w_bc")[:, g * 96:(g + 1) * 96], u[:, cols(h, k, Q)])
                    last.then_inc(s["bc_ready"], 1)
                return stage

            def hidden(r):
                h, k = r // 4, r % 4

                def stage(b, p):
                    if r == 0:
                        pe.wait_ge(s["route_step"], b * RS + 1)
                    elif r == 4:
                        pe.wait_ge(s["fin_ready"], b * 2 + 1)
                    else:
                        pe.wait_ge(s["hid_copied"], b * 8 + r)
                    for c in range(2):
                        last = mm(side[:, c, 0:Q], w("w1")[lo(h), k * 128:(k + 1) * 128], xf[lo(h), c * Q:(c + 1) * Q])
                    last.then_inc(s["hid_ready"], 1)
                return stage

            def pick(r):
                h, k = r // 4, r % 4

                def stage(b, p):
                    if r == 0:
                        pe.wait_ge(s["combT_ready"], b * 2 + 2)
                    elif r == 4:
                        pe.wait_ge(s["hid_copied"], b * 8 + 8)
                    else:
                        pe.wait_ge(s["gated_ready"], b * 8 + r)
                    for c in range(2):
                        last = mm(side[:, c, 0:Q], w("pick")[:, k * 128:(k + 1) * 128], combT[:, cols(h, c, Q)])
                    last.then_inc(s["pick_ready"], 1)
                return stage

            for r in range(NR):
                work[f"bc{r}"] = bc(r)
            for r in range(8):
                work[f"hid{r}"], work[f"pick{r}"] = hidden(r), pick(r)

            def spread_last(row, p, name):
                for n in range(DST):
                    o = n % (DST // 2) * BI
                    last = mm(side[:, n // (DST // 2), o:o + BI], sel[:, row + n % GR, :],
                              last_of(stack[:, p, n // GR, :]))
                last.then_inc(s[name], 1)

            def tail_B(b, p):
                pe.wait_ge(s["outT_ready"], b + 1)
                pe.wait_ge(s["bc_copied"], (b + 2 if not isinstance(b, int) else min(b + 2, NBLK)) * NR)
                spread_last(0, p, "tailB_ready")

            def tail_C(b, p):
                pe.wait_ge(s["tail_dBu"], b + 1)
                spread_last(GR, p, "tailC_ready")

            def proj(b, p):
                pe.wait_ge(s["yg_ready"], b + 1)
                pe.wait_ge(s["yg_last"], b + 1)
                for h in range(2):
                    for c in range(2):
                        last = mm(side[lo(h), c, 0:Q], w_out_half[:, :], yg[:, cols(h, c, Q)])
                last.then_inc(s["proj_ready"], 1)

            def idft(b, p):
                pe.wait_ge(s["gmat_ready"], b * 2 + 2)
                for e in range(HI):
                    last = mm(side[:, e // IQ, (e % IQ) * L:(e % IQ + 1) * L],
                              gmat[:, e, :, :].rearrange("p h c -> p (h c)"), w("idft"))
                last.then_inc(s["ff_ready"], 1)

            def logits(b, p):
                pe.wait_ge(s["post_done"], b * 2 + 2)
                for img in range(BI):
                    h, t = img // HI, (img % HI) * L
                    last = mm(side[0:L, h, (img % HI) * NE:(img % HI + 1) * NE], xf[lo(h), t:t + L],
                              w("router")[lo(h), :])
                last.then_inc(s["logits_ready"], 1)

            def out_turn(b, p):
                pe.wait_ge(s["fin_ready"], b * 2 + 2)
                for e in range(HI):
                    last = pe.transpose(side[0:L, e // IQ, (e % IQ) * 128:(e % IQ + 1) * 128],
                                        fin[:, e * L:(e + 1) * L], w("ident"))
                last.then_inc(s["out_turned"], 1)

            work |= dict(turn=turn, tail_B=tail_B, tail_C=tail_C, proj=proj, idft=idft, logits=logits,
                         out_turn=out_turn)

            def spread(N, n, p):
                g, r = n // GR, n % GR
                if not isinstance(N, int) or N >= 1:
                    pe.wait_ge(s["dBu_done"], N)
                for c in range(2):
                    last = mm(psB[:, c, :], sel[:, r, :], head(stack[:, p, g, :])[:, c * HI:(c + 1) * HI, :])
                last.then_inc(s["B_ready"], 1)
                pe.wait_ge(s["q_done"], N + NBUF)
                for c in range(2):
                    last = mm(psC[:, c, :], sel[:, GR + r, :], head(stack[:, p, g, :])[:, c * HI:(c + 1) * HI, :])
                last.then_inc(s["C_ready"], 1)

            def add_up(N, p, c):
                if c == 0:
                    pe.wait_ge(s["z_done"], N + 1 + NBUF)
                last = mm(psY[:, c, :], half_ident[:, :], z[:, p, c * BANK:(c + 1) * BANK], start=False, stop=False)
                if c == 1:
                    last.then_inc(s["y_added"], 1)

            def iteration(i, ip, pre, post):
                N0 = i * DST
                pe.wait_ge(s["split_step"], (i + 1) * NR * 3)
                for n in range(2):
                    spread(N0 + n, n, ip)
                if post:
                    for n in (2, 1):
                        for c in range(2):
                            add_up(N0 - n, n % 2, c)
                for n in range(DST):
                    if n + 2 < DST:
                        spread(N0 + n + 2, n + 2, ip)
                    if n == 0:
                        if post:
                            pe.wait_ge(s["yg_ready"], i)
                        for c in range(2):
                            mm(psY[:, c, :], diagD[:, :], head(u[:, :])[:, c * HI:(c + 1) * HI, :], stop=False)
                    side_work_at(3 * n, -5, work, i, ip, pre, post)
                    if n + 2 < DST:
                        add_up(N0 + n, n % 2, 0)
                    side_work_at(3 * n + 1, -5, work, i, ip, pre, post)
                    if n + 2 < DST:
                        add_up(N0 + n, n % 2, 1)
                    side_work_at(3 * n + 2, -5, work, i, ip, pre, post)

            side_work_alone(PRE, work, 0, 0)
            iterations(pe, iteration)
            for n in (2, 1):
                for c in range(2):
                    add_up(NBLK * DST - n, n % 2, c)
            side_work_alone(EARLY + LATE, work, NBLK - 1, 1)


def host_pack(inp):
    import numpy as np

    def twice(v):
        return np.concatenate([v, v], axis=0)

    def col(name):
        return np.reshape(inp[name], (-1, 1))

    ident = np.eye(128, dtype=np.float32)
    block_avg = np.kron(np.eye(2), np.full((CH, CH), 1.0 / CH)).astype(np.float32)
    l, f = np.arange(L)[:, None], np.arange(NFREQ)[None, :]
    ang = 2 * np.pi * ((l * f) % L) / L
    dft = np.concatenate([np.cos(ang), -np.sin(ang)], axis=1) / np.sqrt(L)
    weight = np.where(f == 0, 1.0, 2.0)
    idft = np.concatenate([weight * np.cos(ang), -weight * np.sin(ang)], axis=1).T / np.sqrt(L)
    pick = np.kron(np.eye(NE), np.ones((1, CH)))
    A = "L0_attn_"
    w_bc = inp[A + "w_xproj"]
    groups = []
    for g in range(NG):
        b = w_bc[:, DTR + g * GR:DTR + (g + 1) * GR]
        c = w_bc[:, DTR + DST + g * GR:DTR + DST + (g + 1) * GR]
        groups += [b, c] * 3
    w1 = inp["L0_ffn_w1"].reshape(4, 2, CH, CH).transpose(2, 0, 1, 3).reshape(CH, 4 * 128)
    w2 = inp["L0_ffn_w2"].reshape(4, 2, CH, CH).transpose(1, 2, 0, 3).reshape(128, 4 * CH)
    parts = dict(
        tok=np.concatenate([inp["L0_tok_W"], col("L0_tok_b")], axis=1), ident=ident, center=ident - block_avg,
        avg=block_avg, w_in=twice(inp[A + "w_in"]), conv_w=inp[A + "conv_w"].T, conv_b=col(A + "conv_b"),
        b_dt=col(A + "b_dt"), D=col(A + "D"), rb=col(A + "rb"), ib=col(A + "ib"), cls=twice(col("cls_tok")),
        b1=inp["L0_ffn_b1"].reshape(4, 128).T, A_log=inp[A + "A_log"], w_dtr=w_bc[:, 0:DTR],
        w_bc=np.concatenate(groups, axis=1), w_dt=inp[A + "w_dt"], onehot=np.tile(np.eye(32), (3, 1)),
        w_out=inp[A + "w_out"], fc1=twice(inp[A + "fc1_w"]), bn1_s=np.broadcast_to(inp[A + "bn1_s"], (128, 128)),
        bn1_b=np.tile(inp[A + "bn1_b"], 4)[None], Wr=inp[A + "Wr"], Wi=inp[A + "Wi"], fc2=inp[A + "fc2_w"],
        dft=dft, idft=idft, router=twice(inp["L0_ffn_router_w"].T), w1=twice(w1), w2=w2, b2=inp["L0_ffn_b2"],
        pick=pick, rank=np.broadcast_to(NE - np.arange(NE), (128, NE)))
    for name in ("ln1_g", "ln1_b", "mln_g", "mln_b", "ln2_g", "ln2_b", "bn2_s", "bn2_b"):
        parts[name] = twice(col(A + name))
    packed = np.zeros((128, PACK_COLS), np.float32)
    for name, (cols, rows) in PACK.items():
        packed[0:rows, PACK_AT[name]:PACK_AT[name] + cols] = parts[name]
    return packed


def kernel(**inputs):
    import numpy as _np
    import concourse.bacc as _bacc
    from concourse import mybir as _mybir
    from concourse.bass_utils import run_bass_kernel_spmd as _run

    inp = {k: _np.asarray(v) for k, v in inputs.items()}
    arrays = {"x_dram": _np.ascontiguousarray(inp["x"]), "packed_dram": host_pack(inp)}
    nc = _bacc.Bacc("TRN2", target_bir_lowering=False, num_devices=1)
    x, packed = (nc.dram_tensor(k, v.shape, _mybir.dt.from_np(v.dtype), kind="ExternalInput").ap()
                 for k, v in arrays.items())
    out = nc.dram_tensor("out_dram", (NIMG, L, CH), F32, kind="ExternalOutput").ap()
    build(nc, x, packed, out)
    r = _run(nc, [arrays], core_ids=[0])
    return r.results[0]["out_dram"]
```

```python
from contextlib import ExitStack

import concourse.bass as bass
from concourse import mybir

F32 = mybir.dt.float32
BF16 = mybir.dt.bfloat16
ALU = mybir.AluOpType
ACT = mybir.ActivationFunctionType
AX_X = mybir.AxisListType.X

NIMG, GRID, CH = 128, 64, 64
NF = 4
L = GRID + 1
DIN = 2 * CH
DTR, DST, DCONV = CH // 16, 48, 4
NE = 8
NFREQ = L // 2 + 1
BI = 16
HI = BI // 2
NBLK = NIMG // BI
T = BI * L
TH = HI * L
Q = T // 4
IQ = BI // 4
NG, GR = 3, 16
BANK = 512
TM = BI * GRID
ROOM = 7376

EARLY = """yg:4 tail_B:5 tail_A:5 tail_a:5 tail_dBu:6 tail_C:6 tail_ax:6 tail_x:6 tail_z:9 tail_y:9 tail_yd:9
    yg_last:9 proj:10 x1:11 hx:11 hx_b:11""".split()
PRE = """tok_a:11 tok_b:11 turn:12 h_out:12 ln0_c:13 ln0_s:13 ln0_v:14 ln0_r:14 ln0_d:14 ln1_c:14 ln1_s:16 ln1_v:18
    ln1_r:19 ln1_d:22 ln1_a:22 ln2_c:22 ln2_s:23 ln2_v:23 ln2_r:23 ln2_d:25 ln2_a:25 res0:25 res0_t:26 res0_g:27
    res1:28 res1_t:29 res1_g:29 cv0_a:31 cv0_b:31 cv0_t:32 cv0_u:32 cv1_a:33 cv1_b:33 cv1_t:34 cv1_u:35 v0:35
    v0_abs:37 v1:37 v0_exp:38 v0_rnd:38 v0_err:40 v0_log:40 v0_sum:40 v0_du:44 v1_abs:44 bc0:44 v1_exp:44 v1_rnd:47
    v1_err:47 v1_log:49 v1_sum:51 bc0_out:51 bc0_rest:54 dsum:54 v1_du:54 bc0_mid:54 bc1:54 bc0_low:54 bc1_out:54
    bc1_rest:54 bc1_mid:55 bc2:55 bc1_low:55 bc2_out:57 bc2_rest:57 bc2_mid:58 bc3:58 bc2_low:59 bc3_out:61
    bc3_rest:63 bc3_mid:64 bc4:64 bc3_low:66 bc4_out:66 bc4_rest:66 bc4_mid:67 bc5:67 bc4_low:67 bc5_out:67
    bc5_rest:67 bc5_mid:72 bc5_low:72""".split()
LATE = """ln3_c:75 ln3_s:76 ln3_v:78 ln3_r:78 ln3_d:79 f0_a:81 f0_b:81 f0_out:81 dft0:83 dft0_out:83 mix0:84
    mix0_out:87 fc20:87 fc20_out:87 f1_a:88 f1_b:88 f1_out:90 dft1:90 dft1_out:90 mix1:91 mix1_out:91 fc21:92
    fc21_out:92 idft:94 hA:95 ln4_c:96 ln4_s:97 ln4_v:98 ln4_r:98 ln4_d:100 hx2:100 logits:101 logits_out:101
    hid0:101 hid0_out:102 route0:102 hid1:103 hid1_out:103 route1:104 hid2:105 hid2_out:105 route2:106 hid3:106
    hid3_out:107 route3:107 gelu0:107 pair_exp:107 route4:110 route5:110 comb0:110 comb0_out:110 comb1:111
    comb1_out:111 pick0:113 gate0:114 pick1:114 gate1:114 pick2:115 gate2:115 pick3:116 gate3:116 acc0_a:117
    acc0_b:119 fin0:120 hid4:121 hid4_out:121 hid5:122 hid5_out:122 hid6:125 hid6_out:127 hid7:130 hid7_out:131
    gelu1:131 pick4:131 gate4:134 pick5:134 gate5:135 pick6:135 gate6:135 pick7:135 gate7:135 acc1_a:136 acc1_b:136
    fin1:137 out_turn:137 out_out:143""".split()
TURNS = [(name, int(turn)) for name, turn in (entry.split(":") for entry in EARLY + PRE + LATE)]
EARLY, PRE, LATE = ([entry.split(":")[0] for entry in stages] for stages in (EARLY, PRE, LATE))
STAGES = EARLY + PRE + LATE
LOG_EXP = "natural_log_exp_and_others"
NBUF, NX = 2, 3
HALF_LN = 13.815510557964274

PACK = dict(
    tok=(NF + 1, 128), ident=(128, 128), center=(128, 128), avg=(128, 128), w_in=(256, 128),
    conv_b=(1, 128), b_dt=(1, 128), D=(1, 128), rb=(1, 128), ib=(1, 128), ln1_g=(1, 128), ln1_b=(1, 128),
    mln_g=(1, 128), mln_b=(1, 128), ln2_g=(1, 128), bn2_s=(1, 128), bn2_b=(1, 128), cls=(1, 128),
    b1=(4, 128), A_log=(DST, 128), w_dtr=(128, DTR), w_bc=(NG * 96, 128), w_dt=(128, DTR), Wr=(128, 128),
    Wi=(128, 128), fc2=(CH, 128), dft=(2 * NFREQ, L), idft=(L, 2 * NFREQ), router=(NE, 128), w1=(4 * 128, 128),
    w2=(4 * CH, 128), b2=(CH, 3 * NE), rank=(NE, 128),
    ln2_b=(96, CH), fc1=(128, 128), bn1_s=(128, 128), w_out=(CH, 128), conv_w=(DCONV * DIN, 128), onehot=(32, 96),
    bn1_b=(BANK, 96), pick=(4 * 128, 3 * NE))
PACK_AT = {}
_at = 0
for _name, (_w, _) in PACK.items():
    PACK_AT[_name] = _at
    _at += _w
PACK_COLS = _at
KEPT = PACK_AT["ln2_b"]


def build(nc, x, packed, out):
    with ExitStack() as ctx:
        def sb(name, shape, dt=F32):
            return ctx.enter_context(nc.sbuf_tensor(name, shape, dt))

        def sem(name):
            return ctx.enter_context(nc.semaphore(name))

        pack = sb("pack", [128, KEPT])
        room = sb("room", [128, ROOM])

        def w(name):
            cols, rows = PACK[name]
            home, at = (pack, PACK_AT[name]) if PACK_AT[name] < KEPT else (room, PACK_AT[name] - KEPT)
            return home[0:rows, at:at + cols]

        eps_col = sb("eps_col", [128, 4])
        credit = sb("credit", [128, 16])
        mean_h = sb("mean_h", [128, 128])
        tokw = sb("tokw", [128, NF + 1])
        Aneg = sb("Aneg", [128, DST])
        Ahalf = sb("Ahalf", [128, DST])
        half_ident = sb("half_ident", [128, 128])
        diagD = sb("diagD", [128, 128])
        w_conv = sb("w_conv", [128, DCONV, DIN])
        w_v = sb("w_v", [128, DIN])
        conv_bh = sb("conv_bh", [128, 1])
        w_out_half = sb("w_out_half", [128, CH])
        fc1s = sb("fc1s", [128, 128])
        negWi = sb("negWi", [128, 128])
        sel = sb("sel", [96, 32, 128], BF16)
        ident16 = sb("ident16", [L, L], BF16)
        pick16 = sb("pick16", [3 * NE, 4 * 128], BF16)
        bias3 = sb("bias3", [96, BANK], BF16)
        ones3 = sb("ones3", [96, L], BF16)
        not_last = sb("not_last", [128, BI, L], BF16)

        delta = sb("delta", [128, 2, T + 1])
        dsum = sb("dsum", [128, 2, T])
        du = sb("du", [128, 2, T])
        gate2 = sb("gate2", [128, 2, T])
        stack = sb("stack", [96, 2, NG, T], BF16)
        H = sb("H", [128, 2, TH])
        x0 = sb("x0", [128, 2, TH])
        u = sb("u", [128, T])
        u_last = sb("u_last", [128, 2, BI])
        a = sb("a", [128, 2, BI, GRID])
        m = sb("m", [128, 2, TM])
        q = sb("q", [128, NX, TM])
        xs = sb("xs", [128, NX, TM])
        z = sb("z", [128, NX, TM])
        x_end = sb("x_end", [128, 2, DST, BI])
        a_last = sb("a_last", [128, DST, BI])
        dBu_last = sb("dBu_last", [128, DST, BI])
        y_last = sb("y_last", [128, BI])
        yg = sb("yg", [128, T])
        x1 = sb("x1", [128, TH])
        hx = sb("hx", [128, TH])
        xin = sb("xin", [128, 4, 2, CH * NF])
        outT = sb("outT", [L, HI, 2, CH])
        ln_c = sb("ln_c", [128, TH])
        ln_sq = sb("ln_sq", [128, TH])
        ln_r = sb("ln_r", [128, TH])
        ln_y = ln_sq
        bias, bias_rest = ln_c[0:96, 0:BANK], ln_sq[0:64, 0:BANK]
        comb3 = sb("comb3", [L, BI, 3, NE], BF16)
        combT3 = sb("combT3", [3 * NE, T], BF16)
        used = {"pre": 0, "post": 0}

        def share(who, cols, rows=128):
            o = used[who]
            used[who] += cols
            assert used[who] <= ROOM, (who, used[who])
            return room[0:rows, o:o + cols]

        tokT = share("pre", 2 * 4 * CH).rearrange("p (k j) -> p k j", j=CH)
        h1 = share("pre", TH)
        h2 = share("pre", HI * (L + DCONV - 1)).rearrange("p (e l) -> p e l", e=HI)
        th = share("pre", TH)
        vh = share("pre", TH)
        s_relu = [share("pre", TH), share("pre", TH)]
        s_abs = [share("pre", TH), share("pre", TH)]
        s_exp = [share("pre", TH), th]
        s_log = [share("pre", TH), vh]
        pf = share("pre", 2 * TH, 64).rearrange("p (k c) -> p k c", k=2)
        rest = [share("pre", TH, 64), h1[0:64]]

        h3 = share("post", TH)
        fin = share("post", TH)
        hA = share("post", TH)
        xf = share("post", TH)
        combT = share("post", T, 3 * NE)
        lg, lg2, eq, key, oh1, oh2, comb, comb_rest = (
            share("post", BI * NE, L).rearrange("p (e x) -> p e x", x=NE) for _ in range(8))
        stat = share("post", 8 * BI, L).rearrange("p (k e) -> p k e", e=BI)
        both = used["post"]
        fT = share("post", 2 * BANK, L)
        ri = share("post", HI * 2 * NFREQ).rearrange("p (e f) -> p e f", e=HI)
        xx = share("post", HI * 2 * NFREQ).rearrange("p (e f) -> p e f", e=HI)
        gmat = share("post", 2 * BANK, 2 * NFREQ).rearrange("p (e h c) -> p e h c", e=HI, h=2)
        used["post"] = both
        hid = share("post", 4 * TH).rearrange("p (k c) -> p k c", k=4)

        ps = ctx.enter_context(nc.psum_tensor("ps", [128, 8, BANK], F32))
        psY, psB, psC, side = ps[:, 0:2, :], ps[:, 2:4, :], ps[:, 4:6, :], ps[:, 6:8, :]

        def two(t2d, c=Q):
            return t2d.rearrange("p (b c) -> p b c", c=c)

        def quarter(t2d, c):
            return t2d.rearrange("p (h c q) -> p h c q", h=2, q=Q)[:, :, c, :]

        def img(t2d):
            return t2d.rearrange("p (e l) -> p e l", l=L)

        def head(t2d):
            return t2d.rearrange("p (e l) -> p e l", l=L)[:, :, 0:GRID]

        def last_of(t2d):
            return t2d.rearrange("p (e l) -> p e l", l=L)[:, :, GRID]

        def over_n(t2d):
            return t2d.unsqueeze(1).to_broadcast([128, DST, BI])

        names = """packed_in x_in consts_set prepped mask_sel_ready tok_mean tokw_ready A_exp tok_step h_turned h_ready
            pre_centered pre_copied pre_squared pre_var pre_log pre_rstd pre_scaled pre_done post_centered
            post_copied post_squared post_var post_log post_rstd post_done pads_zeroed res_ready res_tanh
            gate_ready conv_ready conv_tanh conv_half u_ready v_weights v_weights_kept fc1_scaled shift_through
            v_ready soft_relu soft_abs soft_exp soft_log soft_round soft_step du_ready dsum_ready bc_ready bc_high
            bc_copied bc_rest bc_middle bc_low u_kept a_ready m_ready B_ready C_ready dBu_done q_done x_done z_done
            y_added x_kept yg_ready tailB_ready tailC_ready tail_A tail_a tail_dBu tail_ax tail_x tail_z tail_y
            tail_yd yg_last proj_ready x1_ready hx_ready f_ready fT_ready dft_ready ri_ready mix_ready xx_ready
            fc2_ready gmat_ready ff_ready hx_shifted hA_ready hx2_ready logits_ready route_step pair_exp
            comb_turned combT_ready combT3_ready hid_ready hid_copied gelu_done pick_ready gated_ready acc_ready
            fin_ready out_turned outT_ready out_stored"""
        s = {n: sem(n) for n in names.split()}
        NPREP = 16
        LNS = {"pre": 3, "post": 2}
        NR = 2 * NG
        RS = 23

        x_v = x.rearrange("(n h k e) i j f -> n (e i) k h (j f)", n=NBLK, h=2, k=4)
        out_v = out.rearrange("(n h e) l c -> n h l e c", n=NBLK, h=2)

        def lo(h):
            return slice(CH * h, CH * h + CH)

        def cols(h, b=0, n=TH):
            return slice(h * TH + b * Q, h * TH + b * Q + n)

        def pre_blocks(b):
            return b + 3 if not isinstance(b, int) else min(b + 3, NBLK)

        def side_work_at(place, offset, work, i, ip, pre, post):
            for name, turn in TURNS:
                if name in work and min(max(turn + offset, 0), 3 * DST - 1) == place:
                    if name in PRE and pre:
                        work[name](i + 1, 1 - ip)
                    if name not in PRE and post:
                        work[name](i - 1, 1 - ip)

        def side_work_alone(names, work, b, p):
            for name in names:
                if name in work:
                    work[name](b, p)

        def iterations(eng, iteration):
            iteration(0, 0, True, False)
            with eng.Fori(0, NBLK // 2 - 1) as j:
                iteration(j * 2 + 1, 1, True, True)
                iteration(j * 2 + 2, 0, True, True)
            iteration(NBLK - 1, 1, False, True)

        block = ctx.enter_context(nc.Block())

        @block.sync
        def _(sp):
            sp.dma_start(pack[:, :], packed[:, 0:KEPT]).then_inc(s["packed_in"], 16)
            sp.dma_start(room[:, 0:PACK_COLS - KEPT], packed[:, KEPT:PACK_COLS]).then_inc(s["packed_in"], 16)
            sp.wait_ge(s["consts_set"], 10)

            def load(b):
                for h in range(2):
                    sp.dma_start(xin[:, :, h, :], x_v[b, :, :, h, :]).then_inc(s["x_in"], 16)

            def store(b):
                sp.wait_ge(s["outT_ready"], b + 2)
                for h in range(2):
                    sp.dma_start(out_v[b, h], outT[:, :, h, :]).then_inc(s["out_stored"], 16)

            load(0)
            sp.wait_ge(s["tok_step"], 1 + NF)
            load(1)
            sp.wait_ge(s["tok_step"], 1 + 2 * NF)
            load(2)
            with sp.Fori(0, NBLK - 3) as j:
                sp.wait_ge(s["tok_step"], j * NF + 1 + 3 * NF)
                load(j + 3)
                store(j)
            for b in range(NBLK - 3, NBLK):
                store(b)
            sp.wait_ge(s["out_stored"], 32 * NBLK + 1)

        @block.gpsimd
        def _(pool):
            for k, v in enumerate((1e-5, 1e-3, 1.0, HALF_LN)):
                pool.memset(eps_col[:, k:k + 1], v).then_inc(s["consts_set"], 1)
            pool.memset(mean_h[:, :], 1.0 / 128).then_inc(s["consts_set"], 1)
            pool.memset(ones3[:, :], 1.0).then_inc(s["consts_set"], 1)
            for p in range(2):
                pool.memset(delta[:, p, T:T + 1], 0.0).then_inc(s["consts_set"], 1)
            pool.memset(not_last[:, :, 0:GRID], 1.0).then_inc(s["consts_set"], 1)
            pool.memset(not_last[:, :, GRID:L], 0.0).then_inc(s["consts_set"], 1)
            credits = ["tok_step", "outT_ready", "out_stored"] + ["q_done"] * NBUF + ["z_done", "x_kept", "y_added"] * NX
            for k, name in enumerate(credits):
                pool.memset(credit[:, k:k + 1], 0.0).then_inc(s[name], 1)
            for p in range(NBUF):
                pool.memset(a[:, p, :, 0:1], 0.0).then_inc(s["x_done"], 1)

            work = {}

            def soft_sum(h):
                def error(b, p):
                    n = b * 2 + h
                    pool.wait_ge(s["soft_round"], n + 1)
                    pool.tensor_tensor(s_abs[h], s_exp[h], s_abs[h], ALU.subtract).then_inc(s["soft_step"], 1)

                def log1p(b, p):
                    n = b * 2 + h
                    pool.wait_ge(s["soft_step"], n * 3 + 1)
                    pool.wait_ge(s["soft_log"], n + 1)
                    pool.tensor_tensor(s_log[h], s_abs[h], s_log[h], ALU.add).then_inc(s["soft_step"], 1)

                def add(b, p):
                    n = b * 2 + h
                    pool.wait_ge(s["soft_step"], n * 3 + 2)
                    pool.tensor_tensor(delta[:, p, cols(h)], s_log[h], s_relu[h], ALU.add).then_inc(s["soft_step"], 1)

                def times_u(b, p):
                    n = b * 2 + h
                    pool.wait_ge(s["soft_step"], n * 3 + 3)
                    pool.tensor_tensor(du[:, p, cols(h)], delta[:, p, cols(h)], u[:, cols(h)], ALU.mult)\
                        .then_inc(s["du_ready"], 1)

                work.update({f"v{h}_err": error, f"v{h}_log": log1p, f"v{h}_sum": add, f"v{h}_du": times_u})

            def split(r):
                g, h = r // 2, r % 2

                def remainder(b, p):
                    n = b * NR + r
                    pool.wait_ge(s["bc_high"], n + 1)
                    pool.wait_ge(s["bc_copied"], n + 1)
                    if r >= 2 or not isinstance(b, int) or b:
                        pool.wait_ge(s["bc_low"], n - 1)
                    pool.tensor_tensor(rest[r % 2], pf[:, r % 2, :], stack[0:64, p, g, cols(h)], ALU.subtract)\
                        .then_inc(s["bc_rest"], 1)

                def low(b, p):
                    pool.wait_ge(s["bc_middle"], b * NR + r + 1)
                    pool.tensor_tensor(stack[0:32, p, g, cols(h)], rest[r % 2][0:32], stack[0:32, p, g, cols(h)],
                                       ALU.subtract).then_inc(s["bc_low"], 1)

                work.update({f"bc{r}_rest": remainder, f"bc{r}_low": low})

            for h in range(2):
                soft_sum(h)
            for r in range(NR):
                split(r)

            def tail_A(b, p):
                pool.wait_ge(s["soft_step"], b * 6 + 6)
                pool.tensor_tensor(a_last[:, :, :], Aneg[:, :].unsqueeze(2).to_broadcast([128, DST, BI]),
                                   over_n(last_of(delta[:, p, 0:T])), ALU.mult).then_inc(s["tail_A"], 1)

            def tail_ax(b, p):
                pool.wait_ge(s["tail_a"], b + 1)
                pool.wait_ge(s["x_kept"], (b + 1) * DST + NX)
                pool.tensor_tensor(a_last[:, :, :], a_last[:, :, :], x_end[:, p, :, :], ALU.mult)\
                    .then_inc(s["tail_ax"], 1)

            def tail_x(b, p):
                pool.wait_ge(s["tail_ax"], b + 1)
                pool.wait_ge(s["tail_dBu"], b + 1)
                pool.tensor_tensor(a_last[:, :, :], a_last[:, :, :], dBu_last[:, :, :], ALU.add)\
                    .then_inc(s["tail_x"], 1)

            def hx_sum(b, p):
                pool.wait_ge(s["x1_ready"], b + 1)
                pool.tensor_tensor(hx[:, :], H[:, p, :], x1[:, :], ALU.add).then_inc(s["hx_ready"], 1)

            def hx2_sum(b, p):
                pool.wait_ge(s["post_done"], b * 2 + 2)
                pool.tensor_tensor(hx[:, :], hA, xf, ALU.add).then_inc(s["hx2_ready"], 1)

            work |= dict(tail_A=tail_A, tail_ax=tail_ax, tail_x=tail_x, hx=hx_sum, hx2=hx2_sum)

            def iteration(i, ip, pre, post):
                for n in range(DST):
                    N, p = i * DST + n, n % NX
                    pool.wait_ge(s["x_done"], N + 1 + NBUF)
                    pool.wait_ge(s["q_done"], N + 1 + NBUF)
                    pool.wait_ge(s["y_added"], N + 1)
                    pool.tensor_tensor(z[:, p, :], q[:, p, :], xs[:, p, :], ALU.mult).then_inc(s["z_done"], 1)
                    for k in range(3):
                        side_work_at(3 * n + k, -4, work, i, ip, pre, post)

            side_work_alone(PRE, work, 0, 0)
            iterations(pool, iteration)
            side_work_alone(EARLY + LATE, work, NBLK - 1, 1)

        @block.scalar
        def _(act):
            act.wait_ge(s["packed_in"], 32)
            act.activation(Ahalf[:, :], w("A_log"), ACT.Exp).then_inc(s["A_exp"], 1)
            act.wait_ge(s["tok_mean"], 1)
            act.activation(tokw[:, :], ps[:, 0, 0:NF + 1], ACT.Copy).then_inc(s["tokw_ready"], 1)
            act.wait_ge(s["v_weights"], 1)
            act.activation(w_v[:, :], ps[:, 1, 0:DIN], ACT.Copy).then_inc(s["v_weights_kept"], 1)
            act.wait_ge(s["consts_set"], 10)
            act.wait_ge(s["prepped"], NPREP)

            work = {}

            def ln(name, which, idx, eps):
                def squares(b, p):
                    n = b * LNS[which] + idx + 1
                    act.wait_ge(s[which + "_centered"], n)
                    act.activation(two(ln_sq[:, :]), side[:, :, 0:Q], ACT.Square).then_inc(s[which + "_squared"], 1)
                    act.activation(two(ln_c[:, :]), side[:, :, 0:Q], ACT.Copy).then_inc(s[which + "_copied"], 1)

                def inverse(b, p):
                    n = b * LNS[which] + idx + 1
                    act.preload_act_table_set(LOG_EXP)
                    act.wait_ge(s[which + "_var"], n)
                    act.activation(two(ln_r[:, :]), side[:, :, 0:Q], ACT.Ln, bias=eps_col[:, eps:eps + 1])\
                        .then_inc(s[which + "_log"], 1)
                    act.wait_ge(s[which + "_log"], n)
                    act.activation(ln_r[:, :], ln_r[:, :], ACT.Exp, scale=-0.5).then_inc(s[which + "_rstd"], 1)

                work[name + "_s"], work[name + "_r"] = squares, inverse

            for k in range(3):
                ln(f"ln{k}", "pre", k, 0 if k == 0 else 1)
            ln("ln3", "post", 0, 1)
            ln("ln4", "post", 1, 0)

            def h_out(b, p):
                act.wait_ge(s["h_turned"], b + 1)
                if not isinstance(b, int) or b >= 2:
                    act.wait_ge(s["hx_ready"], b - 1)
                act.activation(H[:, p, :].rearrange("p (e l) -> p e l", l=L)[:, :, 1:L],
                               side[:, 0, :].rearrange("p (e l) -> p e l", l=GRID), ACT.Copy).then_inc(s["h_ready"], 1)

            work["h_out"] = h_out

            def half_stages(h):
                def res_t(b, p):
                    act.wait_ge(s["res_ready"], b * 2 + h + 1)
                    if h:
                        act.wait_ge(s["gate_ready"], b * 2 + 1)
                    act.activation(two(th), side[:, :, 0:Q], ACT.Tanh, scale=0.5).then_inc(s["res_tanh"], 1)

                def cv_t(b, p):
                    act.wait_ge(s["conv_ready"], b * 2 + h + 1)
                    if h:
                        act.wait_ge(s["u_ready"], b * 2 + 1)
                    act.activation(two(vh), side[:, :, 0:Q], ACT.Identity, bias=conv_bh[:, :], scale=0.5)\
                        .then_inc(s["conv_half"], 1)
                    act.wait_ge(s["gate_ready"], b * 2 + 2)
                    act.activation(two(th), side[:, :, 0:Q], ACT.Tanh, bias=conv_bh[:, :], scale=0.5)\
                        .then_inc(s["conv_tanh"], 1)

                def v_abs(b, p):
                    act.wait_ge(s["v_ready"], b * 2 + h + 1)
                    act.activation(two(s_abs[h]), side[:, :, 0:Q], ACT.Abs, bias=w("b_dt")).then_inc(s["soft_abs"], 1)
                    act.activation(two(s_relu[h]), side[:, :, 0:Q], ACT.Relu, bias=w("b_dt")).then_inc(s["soft_relu"], 1)

                def v_exp(b, p):
                    act.preload_act_table_set(LOG_EXP)
                    act.wait_ge(s["soft_abs"], b * 2 + h + 1)
                    act.activation(s_exp[h], s_abs[h], ACT.Exp, scale=-1.0).then_inc(s["soft_exp"], 1)
                    act.wait_ge(s["soft_exp"], b * 2 + h + 1)
                    act.activation(s_log[h], s_exp[h], ACT.Ln, bias=eps_col[:, 2:3]).then_inc(s["soft_log"], 1)

                def f_out(b, p):
                    act.wait_ge(s["f_ready"], b * 2 + h + 1)
                    if h:
                        act.wait_ge(s["dft_ready"], b * 2 + 1)
                    act.activation(two(fT, BANK), side[0:L, :, :], ACT.Relu).then_inc(s["fT_ready"], 1)

                def dft_out(b, p):
                    act.wait_ge(s["dft_ready"], b * 2 + h + 1)
                    act.activation(ri.rearrange("p (b e) f -> p b (e f)", b=2), side[:, :, 0:4 * 2 * NFREQ], ACT.Copy)\
                        .then_inc(s["ri_ready"], 1)

                def mix_out(b, p):
                    act.wait_ge(s["mix_ready"], b * 2 + h + 1)
                    for c, bias in ((0, "rb"), (1, "ib")):
                        act.activation(xx[:, :, c * NFREQ:(c + 1) * NFREQ],
                                       side[:, c, 0:HI * NFREQ].rearrange("p (e f) -> p e f", f=NFREQ),
                                       ACT.Relu, bias=w(bias)).then_inc(s["xx_ready"], 1)

                def fc2_out(b, p):
                    act.wait_ge(s["fc2_ready"], b * 2 + h + 1)
                    act.activation(gmat[:, h * IQ:(h + 1) * IQ, :, :].rearrange("p e h c -> p h e c"),
                                   side[0:2 * NFREQ, 0, :].rearrange("p (h e c) -> p h e c", h=2, c=CH),
                                   ACT.Copy).then_inc(s["gmat_ready"], 1)

                def gelu(b, p):
                    act.wait_ge(s["hid_copied"], b * 8 + 4 * h + 4)
                    act.activation(hid[:, :, :], hid[:, :, :], ACT.Gelu).then_inc(s["gelu_done"], 1)

                def comb_out(b, p):
                    act.wait_ge(s["comb_turned"], b * 2 + h + 1)
                    act.activation(two(combT3[:, cols(h)]), side[0:3 * NE, :, 0:Q], ACT.Copy)\
                        .then_inc(s["combT3_ready"], 1)
                    act.activation(two(combT[:, cols(h)]), side[0:3 * NE, :, 0:Q], ACT.Copy)\
                        .then_inc(s["combT_ready"], 1)

                work.update({f"res{h}_t": res_t, f"cv{h}_t": cv_t,
                             f"v{h}_abs": v_abs, f"v{h}_exp": v_exp, f"f{h}_out": f_out, f"dft{h}_out": dft_out,
                             f"mix{h}_out": mix_out, f"fc2{h}_out": fc2_out, f"gelu{h}": gelu,
                             f"comb{h}_out": comb_out})

            for h in range(2):
                half_stages(h)

            def bc_out(r):
                g, h = r // 2, r % 2

                def stage(b, p):
                    n = b * NR + r
                    act.wait_ge(s["bc_ready"], n + 1)
                    act.activation(two(stack[:, p, g, cols(h)]), side[0:96, :, 0:Q], ACT.Copy)\
                        .then_inc(s["bc_high"], 1)
                    if r >= 2:
                        act.wait_ge(s["bc_rest"], n - 1)
                    act.activation(two(pf[:, r % 2, :]), side[0:64, :, 0:Q], ACT.Copy).then_inc(s["bc_copied"], 1)
                return stage

            def bc_middle(r):
                g, h = r // 2, r % 2

                def stage(b, p):
                    act.wait_ge(s["bc_rest"], b * NR + r + 1)
                    act.activation(stack[0:64, p, g, cols(h)], rest[r % 2], ACT.Copy).then_inc(s["bc_middle"], 1)
                return stage

            def hid_out(r):
                def stage(b, p):
                    act.wait_ge(s["hid_ready"], b * 8 + r + 1)
                    if r >= 4:
                        act.wait_ge(s["acc_ready"], b * 2 + 1)
                    act.activation(two(hid[:, r % 4, :]), side[:, :, 0:Q], ACT.Identity,
                                   bias=w("b1")[:, r % 4:r % 4 + 1]).then_inc(s["hid_copied"], 1)
                return stage

            for r in range(NR):
                work[f"bc{r}_out"], work[f"bc{r}_mid"] = bc_out(r), bc_middle(r)
            for r in range(8):
                work[f"hid{r}_out"] = hid_out(r)

            def hx_shift(b, p):
                act.wait_ge(s["hx_ready"], b + 1)
                act.activation(hx[:, :], hx[:, :], ACT.Identity, bias=w("bn2_b")).then_inc(s["hx_shifted"], 1)

            def tail_a(b, p):
                act.wait_ge(s["tail_A"], b + 1)
                act.activation(a_last[:, :, :], a_last[:, :, :], ACT.Exp).then_inc(s["tail_a"], 1)

            def pair_exp(b, p):
                act.wait_ge(s["route_step"], b * RS + 13)
                act.activation(stat[:, 5, :], stat[:, 4, :], ACT.Exp).then_inc(s["pair_exp"], 1)

            def out_out(b, p):
                act.wait_ge(s["out_turned"], b + 1)
                act.wait_ge(s["out_stored"], b * 32 + 1)
                act.activation(outT[:, :, :, :].rearrange("p (b e) h c -> p b (e h c)", b=2), side[0:L, :, :],
                               ACT.Copy).then_inc(s["outT_ready"], 1)

            work |= dict(hx_b=hx_shift, tail_a=tail_a, pair_exp=pair_exp, out_out=out_out)

            def keep_end(N, n, p):
                act.activation(x_end[:, p, n, :], xs[:, n % NX, GRID - 1::GRID], ACT.Copy).then_inc(s["x_kept"], 1)

            def iteration(i, ip, pre, post):
                first = isinstance(i, int) and i == 0
                act.wait_ge(s["u_ready"], i * 2 + 2)
                act.activation(u_last[:, ip, :], last_of(u[:, :]), ACT.Copy).then_inc(s["u_kept"], 1)
                act.wait_ge(s["soft_step"], i * 6 + 6)
                act.wait_ge(s["dsum_ready"], i + 1)
                dv = delta[:, ip, 0:T].rearrange("p (e l) -> p e l", l=L)
                for n in range(DST):
                    N, p = i * DST + n, n % 2
                    side_work_at(3 * n, 4, work, i, ip, pre, post)
                    act.wait_ge(s["x_done"], N + 1)
                    if n >= 2:
                        keep_end(N - 2, n - 2, ip)
                    elif not first:
                        keep_end(N - 2, DST + n - 2, 1 - ip)
                    act.activation(a[:, p, :, 1:GRID], dv[:, :, 1:GRID], ACT.Exp, scale=Aneg[:, n:n + 1])\
                        .then_inc(s["a_ready"], 1)
                    side_work_at(3 * n + 1, 4, work, i, ip, pre, post)
                    act.wait_ge(s["q_done"], N + 1)
                    act.activation(m[:, p, :].rearrange("p (e l) -> p e l", l=GRID), head(dsum[:, ip, :]), ACT.Tanh,
                                   scale=Ahalf[:, n:n + 1], bias=eps_col[:, 3:4]).then_inc(s["m_ready"], 1)
                    side_work_at(3 * n + 2, 4, work, i, ip, pre, post)

            side_work_alone(PRE, work, 0, 0)
            iterations(act, iteration)
            for n in (DST - 2, DST - 1):
                N = (NBLK - 1) * DST + n
                act.wait_ge(s["x_done"], N + 1 + NBUF)
                keep_end(N, n, 1)
            side_work_alone(EARLY + LATE, work, NBLK - 1, 1)

        @block.vector
        def _(dve):
            dve.wait_ge(s["packed_in"], 32)
            dve.wait_ge(s["A_exp"], 1)
            dve.tensor_scalar(Aneg[:, :], Ahalf[:, :], -1.0, None, ALU.mult).then_inc(s["prepped"], 1)
            dve.wait_ge(s["prepped"], 1)
            dve.tensor_scalar(Ahalf[:, :], Aneg[:, :], 0.5, None, ALU.mult).then_inc(s["prepped"], 1)
            dve.tensor_scalar(half_ident[:, :], w("ident"), 0.5, None, ALU.mult).then_inc(s["prepped"], 1)
            dve.tensor_scalar(diagD[:, :], w("ident"), w("D"), None, ALU.mult).then_inc(s["prepped"], 1)
            dve.tensor_scalar(conv_bh[:, :], w("conv_b"), 0.5, None, ALU.mult).then_inc(s["prepped"], 1)
            dve.tensor_scalar(w_out_half[:, :], w("w_out"), 0.5, None, ALU.mult).then_inc(s["prepped"], 1)
            dve.tensor_tensor(fc1s[:, :], w("fc1"), w("bn1_s"), ALU.mult).then_inc(s["fc1_scaled"], 1)
            dve.tensor_scalar(negWi[:, :], w("Wi"), -1.0, None, ALU.mult).then_inc(s["prepped"], 1)
            dve.tensor_tensor(w_conv[:, :, :], w("w_in")[:, 0:DIN].unsqueeze(1).to_broadcast([128, DCONV, DIN]),
                              w("conv_w").rearrange("p (k c) -> p k c", c=DIN), ALU.mult).then_inc(s["prepped"], 1)
            dve.tensor_copy(ident16[:, :], w("ident")[0:L, 0:L]).then_inc(s["prepped"], 1)
            dve.tensor_copy(pick16[:, :], w("pick")).then_inc(s["prepped"], 1)
            dve.wait_ge(s["shift_through"], 1)
            dve.tensor_scalar(fc1s[:, :], fc1s[:, :], w("ln2_g"), None, ALU.mult).then_inc(s["prepped"], 1)
            dve.tensor_tensor(bias, w("bn1_b"), ps[0:96, 2, :], ALU.add).then_inc(s["prepped"], 1)
            dve.wait_ge(s["prepped"], NPREP - 4)
            dve.tensor_copy(bias3[:, :], bias).then_inc(s["prepped"], 1)
            dve.wait_ge(s["prepped"], NPREP - 3)
            dve.tensor_tensor(bias_rest, bias[0:64], bias3[0:64, :], ALU.subtract).then_inc(s["prepped"], 1)
            dve.wait_ge(s["prepped"], NPREP - 2)
            dve.tensor_tensor(bias3[0:64, :], bias[0:64], bias3[0:64, :], ALU.subtract).then_inc(s["prepped"], 1)
            dve.wait_ge(s["prepped"], NPREP - 1)
            dve.tensor_tensor(bias3[0:32, :], bias_rest[0:32], bias3[0:32, :], ALU.subtract).then_inc(s["prepped"], 1)
            for p in range(2):
                dve.tensor_copy(H[:, p, :].rearrange("p (e l) -> p e l", l=L)[:, :, 0:1],
                                w("cls").unsqueeze(2).to_broadcast([128, HI, 1])).then_inc(s["mask_sel_ready"], 1)
            dve.tensor_copy(sel[:, :, :], w("onehot").unsqueeze(2).to_broadcast([96, 32, 128]))\
                .then_inc(s["mask_sel_ready"], 1)
            dve.wait_ge(s["tokw_ready"], 1)
            dve.wait_ge(s["consts_set"], 10)

            work = {}
            xv = xin[:, :, :, :].rearrange("p k h (j f) -> p (k h) j f", f=NF)

            def tok(f):
                def stage(b, p):
                    if f == 0:
                        dve.wait_ge(s["x_in"], b * 32 + 32)
                        if not isinstance(b, int) or b >= 2:
                            dve.wait_ge(s["outT_ready"], b - 1)
                            dve.wait_ge(s["bc_low"], b * NR)
                        dve.tensor_scalar(tokT, xv[:, :, :, 0], tokw[:, 0:1], tokw[:, NF:NF + 1], ALU.mult, ALU.add)\
                            .then_inc(s["tok_step"], 1)
                        return
                    dve.wait_ge(s["tok_step"], b * NF + f + 1)
                    dve.scalar_tensor_tensor(tokT, xv[:, :, :, f], tokw[:, f:f + 1], tokT, ALU.mult, ALU.add)\
                        .then_inc(s["tok_step"], 1)
                return stage

            def tok_a(b, p):
                tok(0)(b, p)
                tok(1)(b, p)

            def tok_b(b, p):
                dve.memset(h2[:, :, 0:DCONV - 1], 0.0).then_inc(s["pads_zeroed"], 1)
                tok(2)(b, p)
                tok(3)(b, p)

            def ln(name, which, idx, dst, g=None, beta=None, affine=0):
                def scale(b, p):
                    out = dst(p)
                    n = b * LNS[which] + idx + 1
                    dve.wait_ge(s[which + "_rstd"], n)
                    dve.wait_ge(s[which + "_copied"], n)
                    if g is None:
                        dve.tensor_tensor(out, ln_c[:, :], ln_r[:, :], ALU.mult).then_inc(s[which + "_done"], 1)
                        return
                    dve.scalar_tensor_tensor(ln_y[:, :], ln_c[:, :], w(g), ln_r[:, :], ALU.mult, ALU.mult)\
                        .then_inc(s[which + "_scaled"], 1)

                def shift(b, p):
                    dve.wait_ge(s[which + "_scaled"], b * 2 + affine + 1)
                    dve.tensor_scalar(dst(p), img(ln_y[:, :]), w(beta), None, ALU.add).then_inc(s[which + "_done"], 1)

                work[name + "_d"] = scale
                if g is not None:
                    work[name + "_a"] = shift

            ln("ln0", "pre", 0, lambda p: x0[:, p, :])
            ln("ln1", "pre", 1, lambda p: img(h1), "ln1_g", "ln1_b", 0)
            ln("ln2", "pre", 2, lambda p: h2[:, :, DCONV - 1:], "mln_g", "mln_b", 1)
            ln("ln3", "post", 0, lambda p: h3)
            ln("ln4", "post", 1, lambda p: xf)

            def half_stages(h):
                def res_g(b, p):
                    dve.wait_ge(s["res_tanh"], b * 2 + h + 1)
                    dve.scalar_tensor_tensor(quarter(gate2[:, p, :], h), two(th), 1.0, side[:, :, 0:Q],
                                             ALU.add, ALU.mult).then_inc(s["gate_ready"], 1)

                def cv_u(b, p):
                    dve.wait_ge(s["conv_tanh"], b * 2 + h + 1)
                    dve.wait_ge(s["conv_half"], b * 2 + h + 1)
                    if not isinstance(b, int) or b >= 1:
                        dve.wait_ge(s["u_kept"], b)
                        dve.wait_ge(s["y_added"], (b - 1) * DST + NX + 1)
                    dve.scalar_tensor_tensor(quarter(u[:, :], h), two(th), 1.0, two(vh), ALU.add, ALU.mult)\
                        .then_inc(s["u_ready"], 1)

                def v_rnd(b, p):
                    dve.wait_ge(s["soft_exp"], b * 2 + h + 1)
                    dve.tensor_scalar(s_abs[h], s_exp[h], 1.0, -1.0, ALU.add, ALU.add).then_inc(s["soft_round"], 1)

                def fin_sum(b, p):
                    dve.wait_ge(s["acc_ready"], b * 2 + h + 1)
                    dve.wait_ge(s["hx2_ready"], b + 1)
                    dve.tensor_tensor(fin[:, h * Q:(h + 1) * Q], side[:, 0, 0:Q], hx[:, h * Q:(h + 1) * Q], ALU.add)\
                        .then_inc(s["fin_ready"], 1)

                work.update({f"res{h}_g": res_g, f"cv{h}_u": cv_u, f"v{h}_rnd": v_rnd, f"fin{h}": fin_sum})

            for h in range(2):
                half_stages(h)

            def gate(r):
                def stage(b, p):
                    dve.wait_ge(s["gelu_done"], b * 2 + r // 4 + 1)
                    dve.wait_ge(s["pick_ready"], b * 8 + r + 1)
                    dve.tensor_tensor(two(hid[:, r % 4, :]), side[:, :, 0:Q], two(hid[:, r % 4, :]), ALU.mult)\
                        .then_inc(s["gated_ready"], 1)
                return stage

            for r in range(8):
                work[f"gate{r}"] = gate(r)

            def dsum_scan(b, p):
                dve.wait_ge(s["soft_step"], b * 6 + 6)
                keep = not_last[:, :, :].rearrange("p e l -> p (e l)")
                dve.tensor_tensor_scan(dsum[:, p, ::-1], delta[:, p, T:0:-1], keep[:, ::-1], 0.0, ALU.add, ALU.mult)\
                    .then_inc(s["dsum_ready"], 1)

            def yg_main(b, p):
                dve.wait_ge(s["y_added"], (b + 1) * DST + NX)
                dve.tensor_tensor(head(yg[:, :]), psY.rearrange("p b (e l) -> p (b e) l", l=GRID),
                                  head(gate2[:, p, :]), ALU.mult).then_inc(s["yg_ready"], 1)

            halves = side[:, :, 0:DST // 2 * BI].rearrange("p k (n e) -> p k n e", e=BI)

            def tail_dBu(b, p):
                dve.wait_ge(s["tailB_ready"], b + 1)
                dve.wait_ge(s["du_ready"], b * 2 + 2)
                dve.tensor_tensor(dBu_last[:, :, :].rearrange("p (k n) e -> p k n e", k=2), halves,
                                  last_of(du[:, p, :]).unsqueeze(1).unsqueeze(1).to_broadcast([128, 2, DST // 2, BI]),
                                  ALU.mult).then_inc(s["tail_dBu"], 1)

            def tail_z(b, p):
                dve.wait_ge(s["tailC_ready"], b + 1)
                dve.wait_ge(s["tail_x"], b + 1)
                dve.tensor_tensor(dBu_last[:, :, :].rearrange("p (k n) e -> p k n e", k=2), halves,
                                  a_last[:, :, :].rearrange("p (k n) e -> p k n e", k=2), ALU.mult)\
                    .then_inc(s["tail_z"], 1)

            def tail_y(b, p):
                dve.wait_ge(s["tail_z"], b + 1)
                dve.tensor_reduce(y_last[:, :], dBu_last[:, :, :].rearrange("p n e -> p e n"), AX_X, ALU.add)\
                    .then_inc(s["tail_y"], 1)

            def tail_yd(b, p):
                dve.wait_ge(s["tail_y"], b + 1)
                dve.wait_ge(s["u_kept"], b + 1)
                dve.scalar_tensor_tensor(y_last[:, :], u_last[:, p, :], w("D"), y_last[:, :], ALU.mult, ALU.add)\
                    .then_inc(s["tail_yd"], 1)

            def yg_end(b, p):
                dve.wait_ge(s["tail_yd"], b + 1)
                dve.tensor_tensor(last_of(yg[:, :]), y_last[:, :], last_of(gate2[:, p, :]), ALU.mult)\
                    .then_inc(s["yg_last"], 1)

            def x1_sum(b, p):
                dve.wait_ge(s["proj_ready"], b + 1)
                dve.tensor_tensor(two(x1[:, :]), side[:, :, 0:Q], two(x0[:, p, :]), ALU.add).then_inc(s["x1_ready"], 1)

            def hA_sum(b, p):
                dve.wait_ge(s["ff_ready"], b + 1)
                dve.wait_ge(s["hx_shifted"], b + 1)
                dve.scalar_tensor_tensor(two(hA), side[:, :, 0:Q], w("bn2_s"), two(hx[:, :]), ALU.mult, ALU.add)\
                    .then_inc(s["hA_ready"], 1)

            def wide(k):
                return stat[:, k, :].unsqueeze(2).to_broadcast([L, BI, NE])

            rank = w("rank")[0:L, :].unsqueeze(1).to_broadcast([L, BI, NE])

            def then(b, step, ins):
                ins.then_inc(s["route_step"], 1)
                dve.wait_ge(s["route_step"], b * RS + step)

            def logits_out(b, p):
                dve.wait_ge(s["logits_ready"], b + 1)
                then(b, 1, dve.tensor_copy(lg.rearrange("p (h e) x -> p h (e x)", h=2), side[0:L, :, 0:HI * NE]))

            def route0(b, p):
                then(b, 2, dve.tensor_reduce(stat[:, 0, :], lg, AX_X, ALU.max))
                then(b, 3, dve.tensor_tensor(eq, lg, wide(0), ALU.is_equal))
                then(b, 4, dve.tensor_tensor(key, eq, rank, ALU.mult))

            def route1(b, p):
                then(b, 5, dve.tensor_reduce(stat[:, 1, :], key, AX_X, ALU.max))
                then(b, 6, dve.tensor_tensor(oh1, key, wide(1), ALU.is_equal))
                then(b, 7, dve.scalar_tensor_tensor(lg2, oh1, -1e30, lg, ALU.mult, ALU.add))

            def route2(b, p):
                then(b, 8, dve.tensor_reduce(stat[:, 2, :], lg2, AX_X, ALU.max))
                then(b, 9, dve.tensor_tensor(eq, lg2, wide(2), ALU.is_equal))
                then(b, 10, dve.tensor_tensor(key, eq, rank, ALU.mult))

            def route3(b, p):
                then(b, 11, dve.tensor_reduce(stat[:, 3, :], key, AX_X, ALU.max))
                then(b, 12, dve.tensor_tensor(oh2, key, wide(3), ALU.is_equal))
                then(b, 13, dve.tensor_tensor(stat[:, 4, :], stat[:, 2, :], stat[:, 0, :], ALU.subtract))

            def route4(b, p):
                dve.wait_ge(s["pair_exp"], b + 1)
                then(b, 14, dve.tensor_scalar(stat[:, 6, :], stat[:, 5, :], 1.0, None, ALU.add))
                then(b, 15, dve.reciprocal(stat[:, 6, :], stat[:, 6, :]))
                then(b, 16, dve.tensor_tensor(stat[:, 7, :], stat[:, 5, :], stat[:, 6, :], ALU.mult))
                then(b, 17, dve.tensor_tensor(oh1, oh1, wide(6), ALU.mult))
                then(b, 18, dve.tensor_tensor(oh2, oh2, wide(7), ALU.mult))
                then(b, 19, dve.tensor_tensor(comb, oh1, oh2, ALU.add))

            def route5(b, p):
                then(b, 20, dve.tensor_copy(comb3[:, :, 0, :], comb))
                then(b, 21, dve.tensor_tensor(comb_rest, comb, comb3[:, :, 0, :], ALU.subtract))
                then(b, 22, dve.tensor_tensor(comb3[:, :, 1, :], comb, comb3[:, :, 0, :], ALU.subtract))
                then(b, 23, dve.tensor_tensor(comb3[:, :, 2, :], comb_rest, comb3[:, :, 1, :], ALU.subtract))

            work |= dict(tok_a=tok_a, tok_b=tok_b, dsum=dsum_scan, yg=yg_main, tail_dBu=tail_dBu, tail_z=tail_z,
                         tail_y=tail_y, tail_yd=tail_yd, yg_last=yg_end, x1=x1_sum, hA=hA_sum,
                         logits_out=logits_out, route0=route0, route1=route1, route2=route2, route3=route3,
                         route4=route4, route5=route5)

            def iteration(i, ip, pre, post):
                dve.wait_ge(s["du_ready"], i * 2 + 2)
                for n in range(DST):
                    N, p, px = i * DST + n, n % NBUF, n % NX
                    dve.wait_ge(s["B_ready"], N + 1)
                    dve.wait_ge(s["z_done"], N + 1)
                    dve.wait_ge(s["x_kept"], N + 1)
                    dve.tensor_tensor(xs[:, px, :].rearrange("p (e l) -> p e l", l=GRID),
                                      psB.rearrange("p b (e l) -> p (b e) l", l=GRID), head(du[:, ip, :]), ALU.mult)\
                        .then_inc(s["dBu_done"], 1)
                    side_work_at(3 * n, 0, work, i, ip, pre, post)
                    dve.wait_ge(s["m_ready"], N + 1)
                    dve.wait_ge(s["C_ready"], N + 1)
                    dve.scalar_tensor_tensor(q[:, px, :], m[:, p, :], 1.0, psC.rearrange("p b c -> p (b c)"),
                                             ALU.add, ALU.mult).then_inc(s["q_done"], 1)
                    side_work_at(3 * n + 1, 0, work, i, ip, pre, post)
                    dve.wait_ge(s["a_ready"], N + 1)
                    dve.wait_ge(s["dBu_done"], N + 1)
                    dve.tensor_tensor_scan(xs[:, px, :], a[:, p, :, :].rearrange("p e l -> p (e l)"), xs[:, px, :], 0.0,
                                           ALU.mult, ALU.add).then_inc(s["x_done"], 1)
                    side_work_at(3 * n + 2, 0, work, i, ip, pre, post)

            side_work_alone(PRE, work, 0, 0)
            iterations(dve, iteration)
            side_work_alone(EARLY + LATE, work, NBLK - 1, 1)

        @block.tensor
        def _(pe):
            def mm(o, lhsT, rhs, start=True, stop=True):
                return pe.matmul(o, lhsT, rhs, start=start, stop=stop, skip_group_check=True)

            pe.wait_ge(s["packed_in"], 32)
            pe.wait_ge(s["consts_set"], 10)
            mm(ps[:, 0, 0:NF + 1], mean_h[:, :], w("tok")).then_inc(s["tok_mean"], 1)
            mm(ps[:, 1, 0:DIN], w("w_dtr"), w("w_dt")).then_inc(s["v_weights"], 1)
            pe.wait_ge(s["fc1_scaled"], 1)
            for k in range(4):
                last = mm(ps[0:96, 2, k * 128:(k + 1) * 128], w("ln2_b"), fc1s[0:CH, :])
            last.then_inc(s["shift_through"], 1)
            pe.wait_ge(s["prepped"], NPREP)
            pe.wait_ge(s["mask_sel_ready"], 3)
            pe.wait_ge(s["tokw_ready"], 1)
            pe.wait_ge(s["v_weights_kept"], 1)

            work = {}
            F2 = 2 * NFREQ

            def turn(b, p):
                pe.wait_ge(s["tok_step"], b * NF + 1 + NF)
                if not isinstance(b, int) or b >= 1:
                    pe.wait_ge(s["bc_copied"], b * NR)
                if not isinstance(b, int) or b >= 2:
                    pe.wait_ge(s["x1_ready"], b - 1)
                tv = tokT.rearrange("p (k h) j -> p k (h j)", h=2)
                for k in range(4):
                    last = pe.transpose(side[:, 0, k * 128:(k + 1) * 128], tv[:, k, :], w("ident"))
                last.then_inc(s["h_turned"], 1)

            def ln(name, which, idx, src, ready):
                def center(b, p):
                    ready(b)
                    for c in range(2):
                        last = mm(side[:, c, 0:Q], w("center"), src(p)[:, c * Q:(c + 1) * Q])
                    last.then_inc(s[which + "_centered"], 1)

                def variance(b, p):
                    n = b * LNS[which] + idx + 1
                    pe.wait_ge(s[which + "_squared"], n)
                    pe.wait_ge(s[which + "_copied"], n)
                    for c in range(2):
                        last = mm(side[:, c, 0:Q], w("avg"), ln_sq[:, c * Q:(c + 1) * Q])
                    last.then_inc(s[which + "_var"], 1)

                work[name + "_c"], work[name + "_v"] = center, variance

            def after_pre(b):
                pe.wait_ge(s["bc_copied"], pre_blocks(b) * NR)
                pe.wait_ge(s["bc_low"], pre_blocks(b) * NR)
                pe.wait_ge(s["x1_ready"], b + 1)

            ln("ln0", "pre", 0, lambda p: H[:, p, :], lambda b: pe.wait_ge(s["h_ready"], b + 1))
            ln("ln1", "pre", 1, lambda p: x0[:, p, :], lambda b: pe.wait_ge(s["pre_done"], b * 3 + 1))
            ln("ln2", "pre", 2, lambda p: h1, lambda b: pe.wait_ge(s["pre_done"], b * 3 + 2))
            ln("ln3", "post", 0, lambda p: x1[:, :], after_pre)
            ln("ln4", "post", 1, lambda p: hA, lambda b: pe.wait_ge(s["hA_ready"], b + 1))

            def half_stages(h):
                def res(b, p):
                    if h:
                        pe.wait_ge(s["gate_ready"], b * 2 + 1)
                    else:
                        pe.wait_ge(s["pre_done"], b * 3 + 3)
                    for k in range(2):
                        last = mm(side[:, k, 0:Q], w("w_in")[lo(k), DIN:2 * DIN],
                                  h2[lo(k), h * IQ:(h + 1) * IQ, DCONV - 1:])
                    last.then_inc(s["res_ready"], 1)

                def conv(first):
                    def stage(b, p):
                        if first and h == 0:
                            pe.wait_ge(s["gate_ready"], b * 2 + 2)
                            pe.wait_ge(s["pads_zeroed"], b + 1)
                        if first and h == 1:
                            pe.wait_ge(s["conv_tanh"], b * 2 + 1)
                        for tap in range(DCONV // 2) if first else range(DCONV // 2, DCONV):
                            for k in range(2):
                                last = mm(side[:, k, 0:Q], w_conv[lo(k), tap, :],
                                          h2[lo(k), h * IQ:(h + 1) * IQ, tap:tap + L],
                                          start=(tap == 0), stop=(tap == DCONV - 1))
                        if not first:
                            last.then_inc(s["conv_ready"], 1)
                    return stage

                def v(b, p):
                    pe.wait_ge(s["u_ready"], b * 2 + 2)
                    if h:
                        pe.wait_ge(s["soft_abs"], b * 2 + 1)
                        pe.wait_ge(s["soft_relu"], b * 2 + 1)
                    for k in range(2):
                        last = mm(side[:, k, 0:Q], w_v[:, :], u[:, cols(h, k, Q)])
                    last.then_inc(s["v_ready"], 1)

                def spectral_in(first):
                    def stage(b, p):
                        if first and h == 0:
                            pe.wait_ge(s["post_done"], b * 2 + 1)
                        if first and h == 1:
                            pe.wait_ge(s["gmat_ready"], b * 2 + 1)
                        if first:
                            for k in range(2):
                                mm(side[0:L, k, :], ones3[:, :], bias3[:, :], stop=False)
                        for e in range(IQ // 2) if first else range(IQ // 2, IQ):
                            t = (h * IQ + e) * L
                            for k in range(2):
                                last = mm(side[0:L, k, e * 128:(e + 1) * 128], h3[lo(k), t:t + L], fc1s[lo(k), :],
                                          start=False)
                        if not first:
                            last.then_inc(s["f_ready"], 1)
                    return stage

                def dft(b, p):
                    pe.wait_ge(s["fT_ready"], b * 2 + h + 1)
                    for e in range(HI):
                        last = mm(side[:, e // IQ, (e % IQ) * F2:(e % IQ + 1) * F2], fT[:, e * 128:(e + 1) * 128],
                                  w("dft"))
                    last.then_inc(s["dft_ready"], 1)

                def mix(b, p):
                    pe.wait_ge(s["ri_ready"], b * 2 + h + 1)
                    for c, (wre, wim) in enumerate(((w("Wr"), negWi[:, :]), (w("Wi"), w("Wr")))):
                        mm(side[:, c, 0:HI * NFREQ], wre, ri[:, :, 0:NFREQ], stop=False)
                        last = mm(side[:, c, 0:HI * NFREQ], wim, ri[:, :, NFREQ:F2], start=False)
                    last.then_inc(s["mix_ready"], 1)

                def fc2(b, p):
                    pe.wait_ge(s["xx_ready"], b * 4 + 2 * h + 2)
                    for e in range(HI):
                        last = mm(side[0:F2, 0, e * CH:(e + 1) * CH], xx[:, e, :], w("fc2"))
                    last.then_inc(s["fc2_ready"], 1)

                def comb_turn(b, p):
                    if h:
                        pe.wait_ge(s["combT_ready"], b * 2 + 1)
                        pe.wait_ge(s["combT3_ready"], b * 2 + 1)
                    else:
                        pe.wait_ge(s["route_step"], (b + 1) * RS)
                        pe.wait_ge(s["hid_copied"], b * 8 + 4)
                    for e in range(HI):
                        last = mm(side[0:3 * NE, e // IQ, (e % IQ) * L:(e % IQ + 1) * L],
                                  comb3[:, h * HI + e, :, :].rearrange("p k x -> p (k x)"), ident16[:, :])
                    last.then_inc(s["comb_turned"], 1)

                def accumulate(first):
                    def stage(b, p):
                        if first:
                            pe.wait_ge(s["gated_ready"], b * 8 + 4 * h + 4)
                            for c in range(2):
                                mm(side[lo(c), 0, 0:Q], w("b2"), combT[:, cols(c, h, Q)], stop=False)
                        for k in range(2) if first else range(2, 4):
                            for c in range(2):
                                last = mm(side[lo(c), 0, 0:Q], w("w2")[:, k * CH:(k + 1) * CH],
                                          hid[:, k, c * Q:(c + 1) * Q], start=False, stop=(k == 3))
                        if not first:
                            last.then_inc(s["acc_ready"], 1)
                    return stage

                work.update({f"res{h}": res, f"cv{h}_a": conv(True), f"cv{h}_b": conv(False), f"v{h}": v,
                             f"f{h}_a": spectral_in(True), f"f{h}_b": spectral_in(False), f"dft{h}": dft, f"mix{h}": mix,
                             f"fc2{h}": fc2, f"comb{h}": comb_turn, f"acc{h}_a": accumulate(True),
                             f"acc{h}_b": accumulate(False)})

            for h in range(2):
                half_stages(h)

            def bc(r):
                g, h = r // 2, r % 2

                def stage(b, p):
                    if r == 0:
                        pe.wait_ge(s["soft_abs"], b * 2 + 2)
                        pe.wait_ge(s["soft_relu"], b * 2 + 2)
                    else:
                        pe.wait_ge(s["bc_high"], b * NR + r)
                        pe.wait_ge(s["bc_copied"], b * NR + r)
                    for k in range(2):
                        last = mm(side[0:96, k, 0:Q], w("w_bc")[:, g * 96:(g + 1) * 96], u[:, cols(h, k, Q)])
                    last.then_inc(s["bc_ready"], 1)
                return stage

            def hidden(r):
                h, k = r // 4, r % 4

                def stage(b, p):
                    if r == 0:
                        pe.wait_ge(s["route_step"], b * RS + 1)
                    elif r == 4:
                        pe.wait_ge(s["fin_ready"], b * 2 + 1)
                    else:
                        pe.wait_ge(s["hid_copied"], b * 8 + r)
                    for c in range(2):
                        last = mm(side[:, c, 0:Q], w("w1")[lo(c), k * 128:(k + 1) * 128], xf[lo(c), h * Q:(h + 1) * Q])
                    last.then_inc(s["hid_ready"], 1)
                return stage

            def pick(r):
                h, k = r // 4, r % 4

                def stage(b, p):
                    if r == 0:
                        pe.wait_ge(s["combT_ready"], b * 2 + 2)
                        pe.wait_ge(s["combT3_ready"], b * 2 + 2)
                    elif r == 4:
                        pe.wait_ge(s["hid_copied"], b * 8 + 8)
                    else:
                        pe.wait_ge(s["gated_ready"], b * 8 + r)
                    for c in range(2):
                        last = mm(side[:, c, 0:Q], pick16[:, k * 128:(k + 1) * 128], combT3[:, cols(c, h, Q)])
                    last.then_inc(s["pick_ready"], 1)
                return stage

            for r in range(NR):
                work[f"bc{r}"] = bc(r)
            for r in range(8):
                work[f"hid{r}"], work[f"pick{r}"] = hidden(r), pick(r)

            def spread_last(row, p, name):
                for n in range(DST):
                    o = n % (DST // 2) * BI
                    last = mm(side[:, n // (DST // 2), o:o + BI], sel[:, row + n % GR, :],
                              last_of(stack[:, p, n // GR, :]))
                last.then_inc(s[name], 1)

            def tail_B(b, p):
                pe.wait_ge(s["outT_ready"], b + 1)
                pe.wait_ge(s["bc_copied"], (b + 2 if not isinstance(b, int) else min(b + 2, NBLK)) * NR)
                spread_last(0, p, "tailB_ready")

            def tail_C(b, p):
                pe.wait_ge(s["tail_dBu"], b + 1)
                spread_last(GR, p, "tailC_ready")

            def proj(b, p):
                pe.wait_ge(s["yg_ready"], b + 1)
                pe.wait_ge(s["yg_last"], b + 1)
                for h in range(2):
                    for c in range(2):
                        last = mm(side[lo(h), c, 0:Q], w_out_half[:, :], yg[:, cols(h, c, Q)])
                last.then_inc(s["proj_ready"], 1)

            def idft(b, p):
                pe.wait_ge(s["gmat_ready"], b * 2 + 2)
                for e in range(HI):
                    last = mm(side[:, e // IQ, (e % IQ) * L:(e % IQ + 1) * L],
                              gmat[:, e, :, :].rearrange("p h c -> p (h c)"), w("idft"))
                last.then_inc(s["ff_ready"], 1)

            def logits(b, p):
                pe.wait_ge(s["post_done"], b * 2 + 2)
                for img in range(BI):
                    h, t = img // HI, (img % HI) * L
                    last = mm(side[0:L, h, (img % HI) * NE:(img % HI + 1) * NE], xf[lo(h), t:t + L],
                              w("router")[lo(h), :])
                last.then_inc(s["logits_ready"], 1)

            def out_turn(b, p):
                pe.wait_ge(s["fin_ready"], b * 2 + 2)
                for e in range(HI):
                    last = pe.transpose(side[0:L, e // IQ, (e % IQ) * 128:(e % IQ + 1) * 128],
                                        fin[:, e * L:(e + 1) * L], w("ident"))
                last.then_inc(s["out_turned"], 1)

            work |= dict(turn=turn, tail_B=tail_B, tail_C=tail_C, proj=proj, idft=idft, logits=logits,
                         out_turn=out_turn)

            def spread(N, n, p):
                g, r = n // GR, n % GR
                if not isinstance(N, int) or N >= 1:
                    pe.wait_ge(s["dBu_done"], N)
                for c in range(2):
                    last = mm(psB[:, c, :], sel[:, r, :], head(stack[:, p, g, :])[:, c * HI:(c + 1) * HI, :])
                last.then_inc(s["B_ready"], 1)
                pe.wait_ge(s["q_done"], N + NBUF)
                for c in range(2):
                    last = mm(psC[:, c, :], sel[:, GR + r, :], head(stack[:, p, g, :])[:, c * HI:(c + 1) * HI, :])
                last.then_inc(s["C_ready"], 1)

            def add_up(N, p, c):
                if c == 0:
                    pe.wait_ge(s["z_done"], N + 1 + NX)
                last = mm(psY[:, c, :], half_ident[:, :], z[:, p, c * BANK:(c + 1) * BANK], start=False, stop=False)
                if c == 1:
                    last.then_inc(s["y_added"], 1)

            def iteration(i, ip, pre, post):
                N0 = i * DST
                pe.wait_ge(s["bc_low"], (i + 1) * NR)
                for n in range(2):
                    spread(N0 + n, n, ip)
                if post:
                    for n in (2, 1):
                        for c in range(2):
                            add_up(N0 - n, (DST - n) % NX, c)
                for n in range(DST):
                    if n + 2 < DST:
                        spread(N0 + n + 2, n + 2, ip)
                    if n == 0:
                        if post:
                            pe.wait_ge(s["yg_ready"], i)
                        for c in range(2):
                            mm(psY[:, c, :], diagD[:, :], head(u[:, :])[:, c * HI:(c + 1) * HI, :], stop=False)
                    side_work_at(3 * n, -5, work, i, ip, pre, post)
                    if 1 <= n < DST - 1:
                        add_up(N0 + n - 1, (n - 1) % NX, 0)
                    side_work_at(3 * n + 1, -5, work, i, ip, pre, post)
                    if 1 <= n < DST - 1:
                        add_up(N0 + n - 1, (n - 1) % NX, 1)
                    side_work_at(3 * n + 2, -5, work, i, ip, pre, post)

            side_work_alone(PRE, work, 0, 0)
            iterations(pe, iteration)
            for n in (2, 1):
                for c in range(2):
                    add_up(NBLK * DST - n, (DST - n) % NX, c)
            side_work_alone(EARLY + LATE, work, NBLK - 1, 1)


def host_pack(inp):
    import numpy as np

    def twice(v):
        return np.concatenate([v, v], axis=0)

    def col(name):
        return np.reshape(inp[name], (-1, 1))

    ident = np.eye(128, dtype=np.float32)
    block_avg = np.kron(np.eye(2), np.full((CH, CH), 1.0 / CH)).astype(np.float32)
    l, f = np.arange(L)[:, None], np.arange(NFREQ)[None, :]
    ang = 2 * np.pi * ((l * f) % L) / L
    dft = np.concatenate([np.cos(ang), -np.sin(ang)], axis=1) / np.sqrt(L)
    weight = np.where(f == 0, 1.0, 2.0)
    idft = np.concatenate([weight * np.cos(ang), -weight * np.sin(ang)], axis=1).T / np.sqrt(L)
    pick = np.kron(np.eye(NE), np.ones((1, CH)))
    A = "L0_attn_"
    w_bc = inp[A + "w_xproj"]
    groups = []
    for g in range(NG):
        b = w_bc[:, DTR + g * GR:DTR + (g + 1) * GR]
        c = w_bc[:, DTR + DST + g * GR:DTR + DST + (g + 1) * GR]
        groups += [b, c] * 3
    bn1_b = np.zeros((96, BANK), np.float32)
    bn1_b[0:96:32] = np.tile(inp[A + "bn1_b"], 4)
    ln2_b = np.zeros((CH, 96), np.float32)
    ln2_b[:, 0:96:32] = col(A + "ln2_b")
    w1 = inp["L0_ffn_w1"].reshape(4, 2, CH, CH).transpose(2, 0, 1, 3).reshape(CH, 4 * 128)
    w2 = inp["L0_ffn_w2"].reshape(4, 2, CH, CH).transpose(1, 2, 0, 3).reshape(128, 4 * CH)
    parts = dict(
        tok=np.concatenate([inp["L0_tok_W"], col("L0_tok_b")], axis=1), ident=ident, center=ident - block_avg,
        avg=block_avg, w_in=twice(inp[A + "w_in"]),
        conv_w=np.broadcast_to(inp[A + "conv_w"].reshape(1, -1), (128, DCONV * DIN)), conv_b=col(A + "conv_b"),
        b_dt=col(A + "b_dt"), D=col(A + "D"), rb=col(A + "rb"), ib=col(A + "ib"), cls=twice(col("cls_tok")),
        b1=inp["L0_ffn_b1"].reshape(4, 128).T, A_log=inp[A + "A_log"], w_dtr=w_bc[:, 0:DTR].T,
        w_bc=np.concatenate(groups, axis=1), w_dt=inp[A + "w_dt"], onehot=np.tile(np.eye(32), (3, 1)),
        w_out=inp[A + "w_out"], fc1=twice(inp[A + "fc1_w"]), bn1_s=np.broadcast_to(inp[A + "bn1_s"], (128, 128)),
        bn1_b=bn1_b, ln2_b=ln2_b, Wr=inp[A + "Wr"], Wi=inp[A + "Wi"], fc2=inp[A + "fc2_w"],
        dft=dft, idft=idft, router=twice(inp["L0_ffn_router_w"].T), w1=twice(w1), w2=w2,
        b2=np.tile(inp["L0_ffn_b2"], (3, 1)),
        pick=np.tile(pick, (3, 1)), rank=np.broadcast_to(NE - np.arange(NE), (128, NE)))
    for name in ("ln1_g", "ln1_b", "mln_g", "mln_b", "ln2_g", "bn2_s", "bn2_b"):
        parts[name] = twice(col(A + name))
    packed = np.zeros((128, PACK_COLS), np.float32)
    for name, (cols, rows) in PACK.items():
        packed[0:rows, PACK_AT[name]:PACK_AT[name] + cols] = parts[name]
    return packed


def kernel(**inputs):
    import numpy as _np
    import concourse.bacc as _bacc
    from concourse import mybir as _mybir
    from concourse.bass_utils import run_bass_kernel_spmd as _run

    inp = {k: _np.asarray(v) for k, v in inputs.items()}
    arrays = {"x_dram": _np.ascontiguousarray(inp["x"]), "packed_dram": host_pack(inp)}
    nc = _bacc.Bacc("TRN2", target_bir_lowering=False, num_devices=1)
    x, packed = (nc.dram_tensor(k, v.shape, _mybir.dt.from_np(v.dtype), kind="ExternalInput").ap()
                 for k, v in arrays.items())
    out = nc.dram_tensor("out_dram", (NIMG, L, CH), F32, kind="ExternalOutput").ap()
    build(nc, x, packed, out)
    r = _run(nc, [arrays], core_ids=[0])
    return r.results[0]["out_dram"]
```
